# Optimizing a Trainium2 kernel written in Bass

```python
import numpy as np
import jax
import jax.numpy as jnp

def _softmax(x, axis=-1):
    return jax.nn.softmax(x, axis=axis)

def _gelu(x):
    return jax.nn.gelu(x, approximate=True)

def _silu(x):
    return jax.nn.silu(x)

def _sigmoid(x):
    return jax.nn.sigmoid(x)

def _layernorm(x, axis=-1, eps=1e-05):
    m = jnp.mean(x, axis=axis, keepdims=True)
    v = jnp.var(x, axis=axis, keepdims=True)
    return (x - m) / jnp.sqrt(v + eps)

def _scatter_add(tgt, idx, src, axis=0):
    return tgt.at[idx].add(src)

def _segment_sum(src, seg, n):
    return jax.ops.segment_sum(src, seg, n)
kernel_name = 'mk_sandwich_d1_jaxref_r4_b7694f'

def setup_inputs(seed: int=0):
    np.random.seed(seed)
    _w = jnp.asarray

    def _L0_attn_setup():
        import jax, jax.numpy as jnp
        import numpy as np
        LN_EPS = 1e-05

        def _layernorm(x, g, b):
            m = jnp.mean(x, axis=-1, keepdims=True)
            v = jnp.mean((x - m) ** 2, axis=-1, keepdims=True)
            return (x - m) / jnp.sqrt(v + LN_EPS) * g + b

        def _eigenstate_fft(log_decay, frequency, beta_r, beta_i):
            B, T, K = beta_r.shape
            mag = jax.nn.sigmoid(log_decay)
            n = jnp.arange(T, dtype=beta_r.dtype)
            mag_pow = mag[None, :] ** n[:, None]
            phase = n[:, None] * frequency[None, :]
            kern = mag_pow * (jnp.cos(phase) + 1j * jnp.sin(phase))
            beta = beta_r + 1j * beta_i
            beta_p = jnp.pad(beta, ((0, 0), (0, T), (0, 0)))
            kern_p = jnp.pad(kern, ((0, T), (0, 0)))
            c = jnp.fft.ifft(jnp.fft.fft(beta_p, axis=1) * jnp.fft.fft(kern_p, axis=0)[None], axis=1)[:, :T, :]
            return (c.real.astype(beta_r.dtype), c.imag.astype(beta_r.dtype))

        def _reference_tuple_inner(x, in_proj_w, log_decay, frequency, coupling, out_proj_w, gate_w, gate_b, n1_g, n1_b, n2_g, n2_b, mlp_w1, mlp_b1, mlp_w2, mlp_b2):
            B, T, D = x.shape
            H, Kh, _ = coupling.shape
            K = H * Kh
            xn = _layernorm(x, n1_g, n1_b)
            beta = jnp.einsum('btd,kd->btk', xn, in_proj_w)
            br, bi = (beta[..., :K], beta[..., K:])
            cr, ci = _eigenstate_fft(log_decay, frequency, br, bi)
            cr_h = cr.reshape(B, T, H, Kh)
            ci_h = ci.reshape(B, T, H, Kh)
            cr = jnp.einsum('hjk,bthk->bthj', coupling, cr_h).reshape(B, T, K)
            ci = jnp.einsum('hjk,bthk->bthj', coupling, ci_h).reshape(B, T, K)
            eig = jnp.concatenate([cr, ci], axis=-1)
            out = jnp.einsum('btk,dk->btd', eig, out_proj_w)
            h = jax.nn.sigmoid(jnp.einsum('btd,ed->bte', xn, gate_w) + gate_b) * out
            x = x + h
            x2 = _layernorm(x, n2_g, n2_b)
            hid = jax.nn.silu(jnp.einsum('btd,md->btm', x2, mlp_w1) + mlp_b1)
            x = x + jnp.einsum('btm,dm->btd', hid, mlp_w2) + mlp_b2
            return (x, eig)
        key = jax.random.key(seed)
        ks = jax.random.split(key, 12)
        B, T, D, K, H = (4, 1024, 256, 64, 4)
        Kh = K // H
        M = 4 * D
        f32 = jnp.float32
        inp = {'x': jax.random.normal(ks[0], (B, T, D), f32), 'in_proj_w': jax.random.normal(ks[1], (2 * K, D), f32) / np.sqrt(D), 'log_decay': jax.random.uniform(ks[2], (K,), f32, -3.0, -0.1), 'frequency': jnp.linspace(0.0, 2 * np.pi * (1 - 1.0 / K), K, dtype=f32), 'coupling': jnp.eye(Kh, dtype=f32)[None] + 0.01 * jax.random.normal(ks[3], (H, Kh, Kh), f32) / np.sqrt(Kh), 'out_proj_w': jax.random.normal(ks[4], (D, 2 * K), f32) / np.sqrt(2 * K), 'gate_w': jax.random.normal(ks[5], (D, D), f32) / np.sqrt(D), 'gate_b': jnp.full((D,), -2.0, f32), 'n1_g': jnp.ones((D,), f32), 'n1_b': jnp.zeros((D,), f32), 'n2_g': jnp.ones((D,), f32), 'n2_b': jnp.zeros((D,), f32), 'mlp_w1': jax.random.normal(ks[6], (M, D), f32) / np.sqrt(D), 'mlp_b1': jnp.zeros((M,), f32), 'mlp_w2': jax.random.normal(ks[7], (D, M), f32) / np.sqrt(M), 'mlp_b2': jnp.zeros((D,), f32)}
        return inp
    _L0_attn_in = _L0_attn_setup()

    def _L0_ffn_setup():
        import jax, jax.numpy as jnp
        import numpy as np
        B, S, H, F, G = (8, 512, 256, 1024, 128)
        EPS = 1e-05

        def _dequant(q, scales, g):
            K, N = q.shape
            w = (q.astype(jnp.float32) - 128.0).reshape(K // g, g, N) * scales[:, None, :]
            return w.reshape(K, N)
        key = jax.random.key(seed)
        ks = jax.random.split(key, 8)
        x = jax.random.normal(ks[0], (B, S, H), dtype=jnp.float32)
        ln_gamma = jnp.ones((H,), jnp.float32)
        ln_beta = jnp.zeros((H,), jnp.float32)
        fc1_q = jax.random.randint(ks[1], (H, F), 0, 64, dtype=jnp.int32)
        fc2_q = jax.random.randint(ks[2], (F, H), 0, 64, dtype=jnp.int32)
        fc1_scales = jax.random.uniform(ks[3], (H // G, F), jnp.float32) * 0.02 + 0.001
        fc2_scales = jax.random.uniform(ks[4], (F // G, H), jnp.float32) * 0.02 + 0.001
        fc1_bias = jax.random.normal(ks[5], (F,), jnp.float32) * 0.02
        fc2_bias = jax.random.normal(ks[6], (H,), jnp.float32) * 0.02
        return {'x': x, 'ln_gamma': ln_gamma, 'ln_beta': ln_beta, 'fc1_q': fc1_q, 'fc1_scales': fc1_scales, 'fc1_bias': fc1_bias, 'fc2_q': fc2_q, 'fc2_scales': fc2_scales, 'fc2_bias': fc2_bias}
    _L0_ffn_in = _L0_ffn_setup()
    _d = {'L0_attn_x': _L0_attn_in['x'], 'L0_attn_in_proj_w': _L0_attn_in['in_proj_w'], 'L0_attn_log_decay': _L0_attn_in['log_decay'], 'L0_attn_frequency': _L0_attn_in['frequency'], 'L0_attn_coupling': _L0_attn_in['coupling'], 'L0_attn_out_proj_w': _L0_attn_in['out_proj_w'], 'L0_attn_gate_w': _L0_attn_in['gate_w'], 'L0_attn_gate_b': _L0_attn_in['gate_b'], 'L0_attn_n1_g': _L0_attn_in['n1_g'], 'L0_attn_n1_b': _L0_attn_in['n1_b'], 'L0_attn_n2_g': _L0_attn_in['n2_g'], 'L0_attn_n2_b': _L0_attn_in['n2_b'], 'L0_attn_mlp_w1': _L0_attn_in['mlp_w1'], 'L0_attn_mlp_b1': _L0_attn_in['mlp_b1'], 'L0_attn_mlp_w2': _L0_attn_in['mlp_w2'], 'L0_attn_mlp_b2': _L0_attn_in['mlp_b2'], 'L0_ffn_ln_gamma': _L0_ffn_in['ln_gamma'], 'L0_ffn_ln_beta': _L0_ffn_in['ln_beta'], 'L0_ffn_fc1_q': _L0_ffn_in['fc1_q'], 'L0_ffn_fc1_scales': _L0_ffn_in['fc1_scales'], 'L0_ffn_fc1_bias': _L0_ffn_in['fc1_bias'], 'L0_ffn_fc2_q': _L0_ffn_in['fc2_q'], 'L0_ffn_fc2_scales': _L0_ffn_in['fc2_scales'], 'L0_ffn_fc2_bias': _L0_ffn_in['fc2_bias']}
    _x0 = _d['L0_attn_x']
    _d['L0_attn_x'] = jax.random.normal(jax.random.fold_in(jax.random.key(seed), 1), (4, 2048, 256), dtype=_x0.dtype)
    del _x0
    return _d

def reference(L0_attn_x, L0_attn_in_proj_w, L0_attn_log_decay, L0_attn_frequency, L0_attn_coupling, L0_attn_out_proj_w, L0_attn_gate_w, L0_attn_gate_b, L0_attn_n1_g, L0_attn_n1_b, L0_attn_n2_g, L0_attn_n2_b, L0_attn_mlp_w1, L0_attn_mlp_b1, L0_attn_mlp_w2, L0_attn_mlp_b2, L0_ffn_ln_gamma, L0_ffn_ln_beta, L0_ffn_fc1_q, L0_ffn_fc1_scales, L0_ffn_fc1_bias, L0_ffn_fc2_q, L0_ffn_fc2_scales, L0_ffn_fc2_bias):

    def _L0_attn_ref(x, in_proj_w, log_decay, frequency, coupling, out_proj_w, gate_w, gate_b, n1_g, n1_b, n2_g, n2_b, mlp_w1, mlp_b1, mlp_w2, mlp_b2):
        import jax, jax.numpy as jnp
        import numpy as np
        LN_EPS = 1e-05

        def _layernorm(x, g, b):
            m = jnp.mean(x, axis=-1, keepdims=True)
            v = jnp.mean((x - m) ** 2, axis=-1, keepdims=True)
            return (x - m) / jnp.sqrt(v + LN_EPS) * g + b

        def _eigenstate_fft(log_decay, frequency, beta_r, beta_i):
            B, T, K = beta_r.shape
            mag = jax.nn.sigmoid(log_decay)
            n = jnp.arange(T, dtype=beta_r.dtype)
            mag_pow = mag[None, :] ** n[:, None]
            phase = n[:, None] * frequency[None, :]
            kern = mag_pow * (jnp.cos(phase) + 1j * jnp.sin(phase))
            beta = beta_r + 1j * beta_i
            beta_p = jnp.pad(beta, ((0, 0), (0, T), (0, 0)))
            kern_p = jnp.pad(kern, ((0, T), (0, 0)))
            c = jnp.fft.ifft(jnp.fft.fft(beta_p, axis=1) * jnp.fft.fft(kern_p, axis=0)[None], axis=1)[:, :T, :]
            return (c.real.astype(beta_r.dtype), c.imag.astype(beta_r.dtype))

        def _reference_tuple_inner(x, in_proj_w, log_decay, frequency, coupling, out_proj_w, gate_w, gate_b, n1_g, n1_b, n2_g, n2_b, mlp_w1, mlp_b1, mlp_w2, mlp_b2):
            B, T, D = x.shape
            H, Kh, _ = coupling.shape
            K = H * Kh
            xn = _layernorm(x, n1_g, n1_b)
            beta = jnp.einsum('btd,kd->btk', xn, in_proj_w)
            br, bi = (beta[..., :K], beta[..., K:])
            cr, ci = _eigenstate_fft(log_decay, frequency, br, bi)
            cr_h = cr.reshape(B, T, H, Kh)
            ci_h = ci.reshape(B, T, H, Kh)
            cr = jnp.einsum('hjk,bthk->bthj', coupling, cr_h).reshape(B, T, K)
            ci = jnp.einsum('hjk,bthk->bthj', coupling, ci_h).reshape(B, T, K)
            eig = jnp.concatenate([cr, ci], axis=-1)
            out = jnp.einsum('btk,dk->btd', eig, out_proj_w)
            h = jax.nn.sigmoid(jnp.einsum('btd,ed->bte', xn, gate_w) + gate_b) * out
            x = x + h
            x2 = _layernorm(x, n2_g, n2_b)
            hid = jax.nn.silu(jnp.einsum('btd,md->btm', x2, mlp_w1) + mlp_b1)
            x = x + jnp.einsum('btm,dm->btd', hid, mlp_w2) + mlp_b2
            return (x, eig)
        return _reference_tuple_inner(x, in_proj_w, log_decay, frequency, coupling, out_proj_w, gate_w, gate_b, n1_g, n1_b, n2_g, n2_b, mlp_w1, mlp_b1, mlp_w2, mlp_b2)[0]

    def _L0_ffn_ref(x, ln_gamma, ln_beta, fc1_q, fc1_scales, fc1_bias, fc2_q, fc2_scales, fc2_bias):
        import jax, jax.numpy as jnp
        import numpy as np
        B, S, H, F, G = (8, 512, 256, 1024, 128)
        EPS = 1e-05

        def _dequant(q, scales, g):
            K, N = q.shape
            w = (q.astype(jnp.float32) - 128.0).reshape(K // g, g, N) * scales[:, None, :]
            return w.reshape(K, N)
        residual = x
        mu = jnp.mean(x, axis=-1, keepdims=True)
        var = jnp.mean(jnp.square(x - mu), axis=-1, keepdims=True)
        h = (x - mu) * jax.lax.rsqrt(var + EPS) * ln_gamma + ln_beta
        hf = h.reshape(-1, H)
        w1 = _dequant(fc1_q, fc1_scales, G)
        y = hf @ w1 + fc1_bias
        y = jax.nn.silu(y)
        w2 = _dequant(fc2_q, fc2_scales, G)
        z = y @ w2 + fc2_bias
        return residual + 0.5 * z.reshape(residual.shape)
    x = L0_attn_x
    x = x + _layernorm(_L0_attn_ref(_layernorm(x, axis=-1), L0_attn_in_proj_w, L0_attn_log_decay, L0_attn_frequency, L0_attn_coupling, L0_attn_out_proj_w, L0_attn_gate_w, L0_attn_gate_b, L0_attn_n1_g, L0_attn_n1_b, L0_attn_n2_g, L0_attn_n2_b, L0_attn_mlp_w1, L0_attn_mlp_b1, L0_attn_mlp_w2, L0_attn_mlp_b2), axis=-1)
    x = x + _layernorm(_L0_ffn_ref(_layernorm(x, axis=-1), L0_ffn_ln_gamma, L0_ffn_ln_beta, L0_ffn_fc1_q, L0_ffn_fc1_scales, L0_ffn_fc1_bias, L0_ffn_fc2_q, L0_ffn_fc2_scales, L0_ffn_fc2_bias), axis=-1)
    return x

_drawn_inputs = setup_inputs


def setup_inputs(seed=0):
    import zlib

    import numpy as np

    out = dict(_drawn_inputs(seed))
    spreads = {'L0_attn_gate_b': (-2.0, 0.581),
     'L0_attn_n1_g': (1.0, 0.6),
     'L0_attn_n1_b': (0.0, 0.632),
     'L0_attn_n2_g': (1.0, 0.2),
     'L0_attn_n2_b': (0.0, 0.317),
     'L0_attn_mlp_b1': (0.0, 0.341),
     'L0_attn_mlp_b2': (0.0, 0.1),
     'L0_ffn_ln_gamma': (1.0, 0.2),
     'L0_ffn_ln_beta': (0.0, 0.1)}
    factors = {'L0_attn_log_decay': 3.217, 'L0_ffn_fc1_bias': 64.0, 'L0_ffn_fc2_bias': 64.0}
    for name, (base, spread) in spreads.items():
        noise = np.random.default_rng([zlib.crc32(name.encode()), seed]).standard_normal(out[name].shape)
        drawn = base * np.exp(spread * noise) if base else spread * noise
        out[name] = jnp.asarray(drawn.astype(out[name].dtype))
    for name, factor in factors.items():
        out[name] = (out[name] * factor).astype(out[name].dtype)
    return out
```

```python
from contextlib import ExitStack

import concourse.bass as bass
from concourse import mybir

F32 = mybir.dt.float32
F32R = mybir.dt.float32r
I32 = mybir.dt.int32
ALU = mybir.AluOpType
ACT = mybir.ActivationFunctionType

P = 128
EPS = 1e-5
ROUND_TO_INT = 12582912.0
ROUND_TO_13_BITS = 1536.0
INV_TWO_PI = 0.15915494309189535
TURN = 6.283185


def build(nc, x, in_proj_w, log_decay, frequency, coupling, out_proj_w, gate_w, gate_b, n1_g, n1_b,
          n2_g, n2_b, mlp_w1, mlp_b1, mlp_w2, mlp_b2, ln_gamma, ln_beta, fc1_q, fc1_scales, fc1_bias,
          fc2_q, fc2_scales, fc2_bias, out):
    B, T, D = x.shape
    K2 = in_proj_w.shape[0]
    K = K2 // 2
    H, KH, _ = coupling.shape
    M = mlp_w1.shape[0]
    KT = D // P
    MT = M // P
    PAIRS = MT // 2
    GT = 512
    ST = GT // P
    G = B * T // GT
    GB = T // GT
    SLOTS = 2 * PAIRS
    assert K2 == P and GT == 512 and D == 256 and fc1_q.shape == (D, M) and fc1_scales.shape[0] == KT
    assert GB == 4 and G == 16

    x_rows = x.rearrange("b (g t p) d -> (b g) p t d", t=ST, p=P)
    out_rows = out.rearrange("b (g t p) d -> (b g) p t d", t=ST, p=P)

    with ExitStack() as ctx:
        def sb(name, shape, dt=F32):
            return ctx.enter_context(nc.sbuf_tensor(name, shape, dt))

        def sem(name):
            return ctx.enter_context(nc.semaphore(name))

        win_hi, win_lo = (sb(f"win_{h}", [P, KT, 2, P], F32R) for h in ("hi", "lo"))
        wgate_hi, wgate_lo = (sb(f"wgate_{h}", [P, KT, D], F32R) for h in ("hi", "lo"))
        wout_hi, wout_lo = (sb(f"wout_{h}", [P, 2, D], F32R) for h in ("hi", "lo"))
        wup_hi, wup_lo = (sb(f"wup_{h}", [P, KT, M], F32R) for h in ("hi", "lo"))
        wdown_hi, wdown_lo = (sb(f"wdown_{h}", [P, MT, D], F32R) for h in ("hi", "lo"))
        fup_hi, fup_lo = (sb(f"fup_{h}", [P, KT, M], F32R) for h in ("hi", "lo"))
        fdown_hi, fdown_lo = (sb(f"fdown_{h}", [P, MT, D], F32R) for h in ("hi", "lo"))

        ident = sb("ident", [P, P])
        cos_t = sb("cos_t", [P, T])
        sin_t = sb("sin_t", [P, T])
        decay = sb("decay", [P, GT])
        gate_bias = sb("gate_bias", [P, D])
        vec_bc = sb("vec_bc", [P, 4, D])
        n1_b_bc, n2_b_bc, mlp_b2_bc, fc2_b_bc = (vec_bc[:, k, :] for k in range(4))
        coup = sb("coup", [P, 2, P])
        carry_mask = sb("carry_mask", [P, GB])
        half_power = sb("half_power", [P, 3, ST])
        NROW = 4 * KT + 2 * MT + KT + 2
        vec_rows = sb("vec_rows", [32, P])
        vec_cols = sb("vec_cols", [P, NROW])
        r0 = 0
        cols = {}
        for name, n in (("n1_g", KT), ("n2_g", KT), ("gamma", KT), ("beta", KT), ("b1", MT), ("fb1", MT),
                        ("gate_b", KT), ("log_decay", 1), ("frequency", 1)):
            cols[name] = (r0, n)
            r0 += n

        def col(name, k=0):
            return vec_cols[:, cols[name][0] + k:cols[name][0] + k + 1]

        eps_tile = sb("eps_tile", [P, ST])
        dots = sb("dots", [P, 2 + KT + MT])
        beta_bias = dots[:, 0:2]
        gate_col = sb("gate_col", [P, KT])
        up_bias = sb("up_bias", [P, MT])
        fup_bias = sb("fup_bias", [P, MT])
        tiny = sb("tiny", [P, 8])
        fc2_half = sb("fc2_half", [P, D])

        x_in = sb("x_in", [P, 2, ST, D])
        xn = sb("xn", [P, ST, D])
        xT_hi, xT_lo = (sb(f"xT_{h}", [P, KT, GT], F32R) for h in ("hi", "lo"))
        rot = sb("rot", [P, 2, GT])
        scanned = sb("scanned", [P, GT])
        turned_hi, turned_lo = (sb(f"turned_{h}", [P, 2, GT], F32R) for h in ("hi", "lo"))
        gate = sb("gate", [P, ST, D])
        mid = sb("mid", [P, 4, ST * D])
        x1, x1b, x2n = (mid[:, k, :].rearrange("p (t d) -> p t d", d=D) for k in range(3))
        hid = mid[:, 3, :].rearrange("p (m n) -> p m n", n=GT)
        x1T_hi, x1T_lo = (sb(f"x1T_{h}", [P, KT, GT], F32R) for h in ("hi", "lo"))
        hid_hi, hid_lo = (sb(f"hid_{h}", [P, 2, 2, GT], F32R) for h in ("hi", "lo"))
        late = sb("late", [P, 4, ST * D])
        y = [late[:, k, :].rearrange("p (t d) -> p t d", d=D) for k in range(2)]
        yn, zb = (late[:, k, :].rearrange("p (t d) -> p t d", d=D) for k in (2, 3))
        yT_hi, yT_lo = (sb(f"yT_{h}", [P, KT, GT], F32R) for h in ("hi", "lo"))
        carry = sb("carry", [P, 1])

        y_shift = [sb(f"y_shift{k}", [P, ST]) for k in range(2)]

        class Stat:
            def __init__(self, name, double):
                self.raw = sb(f"{name}_raw", [P, ST, 6])
                self.mv = sb(f"{name}_mv", [P, ST, 2])
                self.var = sb(f"{name}_var", [P, 3, ST])
                self.pow = sb(f"{name}_pow", [P, 3, ST])
                self.neg = sb(f"{name}_neg", [P, ST])
                self.shift = sb(f"{name}_shift", [P, ST])
                self.ratio = sb(f"{name}_ratio", [P, ST])
                self.double = double
                self.bn = sem(f"{name}_bn")
                self.agg = sem(f"{name}_agg")
                self.eps = sem(f"{name}_eps")
                self.powd = sem(f"{name}_powd")
                self.done = sem(f"{name}_done")
                self.r = self.pow[:, 1 if double else 0, :]

        st_x, st_1, st_2, st_y, st_z = (Stat(n, d) for n, d in
                                        (("sx", True), ("s1", False), ("s2", False), ("sy", True), ("sz", False)))

        raw_w1 = mid[:, 0:2, :].rearrange("p a (c d) -> p (a c) d", d=D)
        raw_w2 = mid[:, 2:4, :]
        flat = late[:, :, :].rearrange("p a b -> p (a b)")
        raw_in = flat[:, 0:2 * D].rearrange("p (s d) -> p s d", d=D)
        raw_gate = flat[:, 2 * D:2 * D + KT * D].rearrange("p (e d) -> p e d", d=D)
        raw_out = flat[:, 4 * D:5 * D].rearrange("p (e k) -> p e k", k=P)
        outT = flat[:, 5 * D:6 * D]
        junk = flat[:, 6 * D:7 * D]
        gate_fan = flat[:, 7 * D:8 * D].rearrange("p (e q) -> p e q", q=P)
        tab = [flat[:, 8 * D + k * GT:8 * D + (k + 1) * GT] for k in range(4)]
        q_raw = late[:, 0:2, :].rearrange("p a b -> p (a b)")
        q_scale = late[:, 2:4, :].rearrange("p a b -> p (a b)")

        ps_hid = ctx.enter_context(nc.psum_tensor("ps_hid", [P, 2, 2, GT], F32))
        ps_acc = ctx.enter_context(nc.psum_tensor("ps_acc", [P, ST, D], F32))
        ps_aux = ctx.enter_context(nc.psum_tensor("ps_aux", [P, 2, GT], F32))
        aux_rows = ps_aux[:, :, :].rearrange("p a (s d) -> p (a s) d", d=D)

        rows_in = sem("rows_in")
        small_in = sem("small_in")
        coup_zero = sem("coup_zero")
        w1_in, w2_in = sem("w1_in"), sem("w2_in")
        q1_in, q2_in = sem("q1_in"), sem("q2_in")
        x_loaded = sem("x_loaded")
        stored = sem("stored")
        const_made = sem("const_made")
        ident_zero = sem("ident_zero")
        dve_setup = sem("dve_setup")
        cols_ps, cols_done = sem("cols_ps"), sem("cols_done")
        prep_T = sem("prep_T")
        prep_hi = sem("prep_hi")
        prep_lo = sem("prep_lo")
        outT_done = sem("outT_done")
        fan_done = sem("fan_done")
        dots_done = sem("dots_done")
        gate_bias_made = sem("gate_bias_made")
        gate_bias_ps = sem("gate_bias_ps")
        coup_done = sem("coup_done")
        tables_arg = sem("tables_arg")
        tables_sin = sem("tables_sin")
        decay_tanh = sem("decay_tanh")
        deq_done = sem("deq_done")
        fhi_done = sem("fhi_done")
        flo_done = sem("flo_done")
        fbias_ps = sem("fbias_ps")
        setup_bias = sem("setup_bias")

        xn_done = sem("xn_done")
        xT_ps = sem("xT_ps")
        xT_hid, xT_lod = sem("xT_hid"), sem("xT_lod")
        beta_ps = sem("beta_ps")
        rot_done = sem("rot_done")
        turned_in = sem("turned_in")
        scan_done = sem("scan_done")
        carry_done = sem("carry_done")
        back_done = sem("back_done")
        turned_hid, turned_lod = sem("turned_hid"), sem("turned_lod")
        gate_ps = sem("gate_ps")
        gate_pre = sem("gate_pre")
        gate_done = sem("gate_done")
        out_ps = sem("out_ps")
        gated = sem("gated")
        x1_done = sem("x1_done")
        x1b_done = sem("x1b_done")
        x2n_done = sem("x2n_done")
        x1T_ps = sem("x1T_ps")
        x1T_hid, x1T_lod = sem("x1T_hid"), sem("x1T_lod")
        up_done = sem("up_done")
        act_done = sem("act_done")
        lo_done = sem("lo_done")
        down_done = sem("down_done")
        x2_done = sem("x2_done")
        y_done = sem("y_done")
        yn_done = sem("yn_done")
        yT_ps = sem("yT_ps")
        yT_hid, yT_lod = sem("yT_hid"), sem("yT_lod")
        zb_done = sem("zb_done")
        z_done = sem("z_done")
        z_shift = sem("z_shift")
        y_shift_done = sem("y_shift_done")
        z_scaled = sem("z_scaled")
        out_done = sem("out_done")

        def step(i, s):
            if isinstance(i, int) and (i == 0 or i == G):
                return s if i == 0 else SLOTS * G - 2 * PAIRS + s
            return i * SLOTS + (s - PAIRS)

        def over_rows(vec):
            return vec.unsqueeze(1).to_broadcast([P, ST, D])

        class Stages:
            def __init__(self, front=True, mlp=True, ffn=True, final=True, next_stat=True):
                self.front, self.mlp, self.ffn, self.final, self.next_stat = front, mlp, ffn, final, next_stat

            def slots(self):
                return [s for s in range(SLOTS) if (self.mlp if s < PAIRS else self.ffn)]

        def stages(i):
            return Stages(front=i + 1 < G, mlp=0 <= i < G, ffn=1 <= i <= G, final=2 <= i, next_stat=i + 2 < G)

        LOOP_FROM, LOOP_TO = 2, G - 2

        def run(eng, iteration, second_setup=None):
            for i in range(-1, LOOP_FROM):
                if i == 0 and second_setup:
                    second_setup()
                iteration(i, i % 2, stages(i))
            with eng.Fori(0, (LOOP_TO - LOOP_FROM) // 2) as j:
                for u in range(2):
                    iteration(j * 2 + (LOOP_FROM + u), u, Stages())
            for i in range(LOOP_TO, G + 2):
                iteration(i, i % 2, stages(i))

        block = ctx.enter_context(nc.Block())

        @block.sync
        def _(sp):
            def load_x(n, par):
                sp.dma_start(x_in[:, par, :, :], x_rows[n]).then_inc(x_loaded, 16)

            def rows(name, vec):
                a, n = cols[name]
                sp.dma_start(vec_rows[a:a + n, :], vec.rearrange("(k p) -> k p", p=P)).then_inc(rows_in, 16)

            load_x(0, 0)
            for name, vec in (("n1_g", n1_g), ("n2_g", n2_g), ("gamma", ln_gamma), ("beta", ln_beta),
                              ("b1", mlp_b1), ("fb1", fc1_bias), ("gate_b", gate_b)):
                rows(name, vec)
            for name, vec in (("log_decay", log_decay), ("frequency", frequency)):
                a = cols[name][0]
                for half in range(2):
                    sp.dma_start(vec_rows[a:a + 1, half * K:(half + 1) * K],
                                 vec.rearrange("(a k) -> a k", a=1)).then_inc(rows_in, 16)
            for k, vec in enumerate((n1_b, n2_b, mlp_b2, fc2_bias)):
                sp.dma_start(vec_bc[:, k, :], vec.partition_broadcast(P)).then_inc(rows_in, 16)
            sp.dma_start(raw_in[:, 0, :], in_proj_w).then_inc(small_in, 16)
            sp.dma_start(raw_in[0:K, 1, :], in_proj_w[K:K2, :]).then_inc(small_in, 16)
            sp.dma_start(raw_in[K:K2, 1, :], in_proj_w[0:K, :]).then_inc(small_in, 16)
            sp.dma_start(raw_gate, gate_w.rearrange("(e p) d -> p e d", p=P)).then_inc(small_in, 16)
            sp.dma_start(raw_out, out_proj_w.rearrange("(e p) k -> p e k", p=P)).then_inc(small_in, 16)
            sp.wait_ge(coup_zero, 1)
            for part in range(2):
                for h in range(H):
                    a = part * K + h * KH
                    sp.dma_start(coup[a:a + KH, 0, a:a + KH], coupling[h]).then_inc(small_in, 16)
            sp.dma_start(raw_w1, mlp_w1.rearrange("(c p) d -> p c d", p=P)).then_inc(w1_in, 16)
            sp.dma_start(raw_w2, mlp_w2.rearrange("(e p) m -> p e m", p=P)).then_inc(w2_in, 16)
            sp.wait_ge(st_x.agg, 1)
            load_x(1, 1)
            sp.wait_ge(prep_T, 3)
            sp.wait_ge(gate_bias_ps, 1)
            sp.wait_ge(dots_done, 1)
            sp.wait_ge(tables_sin, 2 * GB)
            sp.dma_start(q_raw.bitcast(I32).rearrange("p (k m) -> p k m", m=M),
                         fc1_q.rearrange("(k p) m -> p k m", p=P)).then_inc(q1_in, 16)
            sp.dma_start(q_scale.rearrange("p (k m) -> p k m", m=M),
                         fc1_scales.partition_broadcast(P)).then_inc(q1_in, 16)
            sp.wait_ge(flo_done, 1)
            sp.wait_ge(fbias_ps, 1)
            sp.dma_start(q_raw.bitcast(I32).rearrange("p (c d) -> p c d", d=D),
                         fc2_q.rearrange("(c p) d -> p c d", p=P)).then_inc(q2_in, 16)
            sp.dma_start(q_scale.rearrange("p (c d) -> p c d", d=D),
                         fc2_scales.partition_broadcast(P)).then_inc(q2_in, 16)

            def iteration(i, par, on):
                if on.final:
                    sp.wait_ge(out_done, i - 1)
                    sp.dma_start(out_rows[i - 2], zb).then_inc(stored, 16)
                if on.mlp and on.next_stat:
                    sp.wait_ge(y_done, i + 1)
                    sp.dma_start(x_in[:, par, :, :], x_rows[i + 2]).then_inc(x_loaded, 16)

            run(sp, iteration)
            sp.wait_ge(stored, 16 * G)

        @block.gpsimd
        def _(pool):
            nc.gpsimd.memset(ident[:], 0.0).then_inc(ident_zero, 1)
            pool.wait_ge(ident_zero, 1)
            nc.gpsimd.affine_select(out=ident[:], in_=ident[:], compare_op=ALU.not_equal, fill=1.0, base=0,
                                    pattern=[[-1, P]], channel_multiplier=1).then_inc(const_made, 1)
            nc.gpsimd.memset(coup[:], 0.0).then_inc(coup_zero, 1)
            nc.gpsimd.memset(eps_tile[:], EPS).then_inc(const_made, 1)
            nc.gpsimd.memset(half_power[:, 0:2, :], -0.5).then_inc(const_made, 1)
            nc.gpsimd.memset(half_power[:, 2:3, :], 0.5).then_inc(const_made, 1)
            nc.gpsimd.memset(carry_mask[:, 0:1], 0.0).then_inc(const_made, 1)
            nc.gpsimd.memset(carry_mask[:, 1:GB], 1.0).then_inc(const_made, 1)
            nc.gpsimd.memset(tiny[:, 4:5], TURN).then_inc(const_made, 1)
            nc.gpsimd.iota(cos_t[:], pattern=[[1, T]], base=0, channel_multiplier=0,
                           allow_small_or_imprecise_dtypes=True).then_inc(const_made, 1)
            pool.wait_ge(const_made, 8)
            nc.gpsimd.memset(tiny[K:K2, 4:5], -TURN).then_inc(const_made, 1)
            pool.wait_ge(const_made, 9)

            def stat(st, n, free):
                pool.wait_ge(st.agg, n + 1)
                free()
                last = nc.gpsimd.tensor_tensor(st.var[:, 0, :], st.mv[:, :, 1], eps_tile[:, :], ALU.add)
                if st.double:
                    for k in (1, 2):
                        last = nc.gpsimd.tensor_scalar(st.var[:, k, :], st.mv[:, :, 1], 1.0 + EPS, EPS * EPS,
                                                       ALU.mult, ALU.add)
                last.then_inc(st.eps, 1)
                nc.gpsimd.tensor_scalar(st.neg[:, :], st.mv[:, :, 0], -1.0, 0.0, ALU.mult, ALU.add)
                k = 3 if st.double else 1
                pool.wait_ge(st.eps, n + 1)
                nc.gpsimd.tensor_tensor(st.pow[:, 0:k, :], st.var[:, 0:k, :], half_power[:, 0:k, :],
                                        ALU.pow).then_inc(st.powd, 1)
                pool.wait_ge(st.powd, n + 1)
                if st.double:
                    nc.gpsimd.tensor_tensor(st.ratio[:, :], st.pow[:, 0, :], st.pow[:, 2, :], ALU.mult)
                nc.gpsimd.tensor_tensor(st.shift[:, :], st.neg[:, :], st.r, ALU.mult).then_inc(st.done, 1)

            def free_x(n):
                def f():
                    if not isinstance(n, int) or n > 0:
                        pool.wait_ge(xn_done, n)
                        pool.wait_ge(x1_done, n)
                return f

            stat(st_x, 0, free_x(0))

            def iteration(i, par, on):
                if on.final:
                    def free_z():
                        if not isinstance(i, int) or i > 2:
                            pool.wait_ge(z_scaled, i - 2)
                    stat(st_z, i - 2, free_z)
                    pool.wait_ge(y_shift_done, i - 1)
                    pool.wait_ge(st_z.done, i - 1)
                    nc.gpsimd.tensor_tensor(st_z.neg[:, :], st_z.shift[:, :], y_shift[par][:, :],
                                            ALU.add).then_inc(z_shift, 1)
                    pool.wait_ge(z_scaled, i - 1)
                    nc.gpsimd.tensor_tensor(zb, zb, y[par], ALU.add).then_inc(out_done, 1)
                if on.front:
                    def free_1():
                        if not isinstance(i, int) or i >= 0:
                            pool.wait_ge(x2n_done, i + 1)
                    stat(st_1, i + 1, free_1)
                if on.mlp:
                    def free_2():
                        if not isinstance(i, int) or i > 0:
                            pool.wait_ge(y_done, i)
                    stat(st_2, i, free_2)
                    nc.gpsimd.tensor_tensor(y_shift[par][:, :], st_2.neg[:, :], st_2.r, ALU.mult).then_inc(
                        y_shift_done, 1)

                    def free_y():
                        if not isinstance(i, int) or i > 0:
                            pool.wait_ge(yn_done, i)
                            pool.wait_ge(zb_done, i)
                    stat(st_y, i, free_y)
                if on.front:
                    pool.wait_ge(x1_done, i + 2)
                    if on.mlp:
                        pool.wait_ge(y_done, i + 1)
                    nc.gpsimd.tensor_tensor(x1b, x1, over_rows(mlp_b2_bc), ALU.add).then_inc(x1b_done, 1)
                if on.next_stat:
                    stat(st_x, i + 2, free_x(i + 2))

            run(pool, iteration)


        @block.tensor
        def _(pe):
            def transpose(dst, src):
                k = src.partition_size()
                return nc.tensor.transpose(dst, src, ident[0:k, 0:k])

            def staged(b):
                return ps_hid[:, b, :, :].rearrange("p a n -> p (a n)")

            pe.wait_ge(const_made, 9)
            pe.wait_ge(rows_in, 16 * 15)
            transpose(ps_aux[:, 0, 0:NROW], vec_rows[0:NROW, :]).then_inc(cols_ps, 1)
            pe.wait_ge(small_in, 16 * (5 + 2 * H))
            for k in range(KT):
                for s in range(2):
                    transpose(staged(0)[:, (2 * k + s) * P:(2 * k + s + 1) * P], raw_in[:, s, k * P:(k + 1) * P])
            for k in range(KT):
                for e in range(KT):
                    last = transpose(staged(0)[:, GT + (2 * k + e) * P:GT + (2 * k + e + 1) * P],
                                     raw_gate[:, e, k * P:(k + 1) * P])
            last.then_inc(prep_T, 1)
            for e in range(KT):
                last = transpose(staged(1)[:, e * P:(e + 1) * P], raw_out[:, e, :])
            last.then_inc(prep_T, 1)
            pe.wait_ge(fan_done, 1)
            for e in range(KT):
                last = nc.tensor.matmul(ps_aux[:, 1, e * P:(e + 1) * P], gate_fan[:, e, :], ident[:],
                                        start=True, stop=True)
            last.then_inc(gate_bias_ps, 1)
            pe.wait_ge(outT_done, 1)
            pe.wait_ge(coup_done, 1)
            for s in range(2):
                last = nc.tensor.matmul(staged(1)[:, GT + s * D:GT + (s + 1) * D], coup[:, s, :], outT,
                                        start=True, stop=True)
            last.then_inc(prep_T, 1)
            pe.wait_ge(w1_in, 16)
            for k in range(KT):
                pe.wait_ge(prep_hi, k + 1)
                pe.wait_ge(prep_lo, k + 1)
                for c in range(MT):
                    last = transpose(staged(k)[:, c * P:(c + 1) * P], raw_w1[:, c, k * P:(k + 1) * P])
                last.then_inc(prep_T, 1)
            pe.wait_ge(w2_in, 16)
            for half in range(2):
                pe.wait_ge(prep_hi, half + 3)
                pe.wait_ge(prep_lo, half + 3)
                for c in range(MT // 2):
                    for e in range(KT):
                        a = e * M + (half * MT // 2 + c) * P
                        last = transpose(staged(half)[:, (KT * c + e) * P:(KT * c + e + 1) * P],
                                         raw_w2.rearrange("p a b -> p (a b)")[:, a:a + P])
                last.then_inc(prep_T, 1)
            pe.wait_ge(prep_hi, 6)
            pe.wait_ge(prep_lo, 6)

            def second_setup():
                pe.wait_ge(deq_done, 1)
                pe.wait_ge(x1T_hid, 1)
                pe.wait_ge(x1T_lod, 1)
                for m in range(MT):
                    for k in range(KT):
                        last = nc.tensor.matmul(ps_aux[:, 0, m:m + 1], q_raw[:, k * M + m * P:k * M + (m + 1) * P],
                                                col("beta", k), start=(k == 0), stop=(k == KT - 1))
                last.then_inc(fbias_ps, 1)

            def turn_rows(src, done):
                for k in range(KT):
                    for t in range(ST):
                        last = transpose(ps_aux[:, k, t * P:(t + 1) * P], src[:, t, k * P:(k + 1) * P])
                last.then_inc(done, 1)

            def three(dst, w_hi, w_lo, a_hi, a_lo, start, stop, **kw):
                nc.tensor.matmul(dst, w_hi, a_hi, start=start, stop=False, **kw)
                nc.tensor.matmul(dst, w_hi, a_lo, start=False, stop=False, **kw)
                return nc.tensor.matmul(dst, w_lo, a_hi, start=False, stop=stop, **kw)

            def rows_product(dst, t, a_hi, a_lo, w_hi, w_lo, first, final):
                return three(dst[:, t, :], a_hi, a_lo, w_hi, w_lo, start=first and t % 2 == 0, stop=final,
                             skip_group_check=True)

            def up(i, s):
                k = step(i, s)
                w_hi, w_lo, a_hi, a_lo = (wup_hi, wup_lo, x1T_hi, x1T_lo) if s < PAIRS else (fup_hi, fup_lo, yT_hi, yT_lo)
                if s == 0:
                    pe.wait_ge(x1T_hid, i + 1)
                    pe.wait_ge(x1T_lod, i + 1)
                if s == PAIRS:
                    pe.wait_ge(yT_hid, i)
                    pe.wait_ge(yT_lod, i)
                    if isinstance(i, int) and i == 1:
                        pe.wait_ge(flo_done, 2)
                if not isinstance(k, int) or k >= 2:
                    pe.wait_ge(act_done, k - 1)
                for h in range(2):
                    m = 2 * (s % PAIRS) + h
                    for c in range(KT):
                        last = three(ps_hid[:, s % 2, h, :], w_hi[:, c, m * P:(m + 1) * P],
                                     w_lo[:, c, m * P:(m + 1) * P], a_hi[:, c, :], a_lo[:, c, :],
                                     start=(c == 0), stop=(c == KT - 1))
                last.then_inc(up_done, 1)

            def down(i, s):
                k = step(i, s)
                w_hi, w_lo = (wdown_hi, wdown_lo) if s < PAIRS else (fdown_hi, fdown_lo)
                first, final = s % PAIRS == 0, s % PAIRS == PAIRS - 1
                if s == 0 and (not isinstance(i, int) or i >= 2):
                    pe.wait_ge(z_done, i - 1)
                if s == PAIRS:
                    if isinstance(i, int) and i == G:
                        pe.wait_ge(z_done, i - 1)
                    else:
                        pe.wait_ge(x2_done, i + 1)
                pe.wait_ge(act_done, k + 1)
                pe.wait_ge(lo_done, k + 1)
                for h in range(2):
                    m = 2 * (s % PAIRS) + h
                    for t in range(ST):
                        tile = slice(t * P, (t + 1) * P)
                        last = rows_product(ps_acc, t, hid_hi[:, s % 2, h, tile], hid_lo[:, s % 2, h, tile],
                                            w_hi[:, m, :], w_lo[:, m, :], first and h == 0, final and h == 1)
                last.then_inc(down_done, 1)

            def iteration(i, par, on):
                n = i + 1
                for s in range(SLOTS):
                    if s in on.slots():
                        up(i, s)
                    if s == 0 and on.ffn:
                        pe.wait_ge(yn_done, i)
                        turn_rows(yn, yT_ps)
                    if s == 1 and on.front:
                        if on.ffn:
                            pe.wait_ge(yT_hid, i)
                            pe.wait_ge(yT_lod, i)
                        if isinstance(i, int) and i == -1:
                            pe.wait_ge(gate_bias_made, 1)
                        if isinstance(i, int) and i == 0:
                            pe.wait_ge(setup_bias, 1)
                        pe.wait_ge(xn_done, n + 1)
                        turn_rows(xn, xT_ps)
                    if s == 2 and on.front:
                        pe.wait_ge(xT_hid, n + 1)
                        pe.wait_ge(xT_lod, n + 1)
                        for w in range(2):
                            for c in range(KT):
                                last = three(ps_aux[:, w, :], win_hi[:, c, w, :], win_lo[:, c, w, :],
                                             xT_hi[:, c, :], xT_lo[:, c, :], start=(c == 0), stop=(c == KT - 1))
                        last.then_inc(beta_ps, 1)
                    if s == 3 and on.front:
                        pe.wait_ge(rot_done, n + 1)
                        for c in range(KT):
                            for t in range(ST):
                                tile = slice(t * P, (t + 1) * P)
                                last = rows_product(aux_rows, t, xT_hi[:, c, tile], xT_lo[:, c, tile],
                                                    wgate_hi[:, c, :], wgate_lo[:, c, :], c == 0, c == KT - 1)
                        last.then_inc(gate_ps, 1)
                    if s == 4 and on.front:
                        pe.wait_ge(gate_pre, n + 1)
                        pe.wait_ge(turned_hid, n + 1)
                        pe.wait_ge(turned_lod, n + 1)
                        for w in range(2):
                            for t in range(ST):
                                tile = slice(t * P, (t + 1) * P)
                                last = rows_product(aux_rows, t, turned_hi[:, w, tile], turned_lo[:, w, tile],
                                                    wout_hi[:, w, :], wout_lo[:, w, :], w == 0, w == 1)
                        last.then_inc(out_ps, 1)
                    if s == 7 and on.front:
                        pe.wait_ge(x2n_done, n + 1)
                        pe.wait_ge(gated, n + 1)
                        turn_rows(x2n, x1T_ps)
                    if s == 0 and on.final:
                        down(i - 1, SLOTS - 1)
                    elif s > 0 and s - 1 in on.slots():
                        down(i, s - 1)

            run(pe, iteration, second_setup)

        @block.scalar
        def _(act):
            def scaled(dst, src, scale=1.0, bias=0.0):
                return nc.scalar.activation(dst, src, ACT.Identity, scale=scale, bias=bias)

            def staged(b):
                return ps_hid[:, b, :, :].rearrange("p a n -> p (a n)")

            act.wait_ge(cols_done, 1)
            nc.scalar.activation(tiny[:, 7:8], col("log_decay"), ACT.Silu)
            nc.scalar.activation(tiny[:, 5:6], col("log_decay"), ACT.Tanh, scale=0.5).then_inc(decay_tanh, 1)
            for q in range(GB):
                part = slice(q * GT, (q + 1) * GT)
                act.wait_ge(const_made, 9)
                act.wait_ge(tables_arg, 2 * q + 1)
                nc.scalar.activation(sin_t[:, part], tab[2], ACT.Sin, scale=tiny[:, 4:5]).then_inc(tables_sin, 1)
                act.wait_ge(tables_arg, 2 * q + 2)
                nc.scalar.activation(cos_t[:, part], tab[3], ACT.Sin, scale=TURN).then_inc(tables_sin, 1)
            act.wait_ge(prep_T, 1)
            for k in range(KT):
                scaled(win_hi[:, k, :, :].rearrange("p s c -> p (s c)"), staged(0)[:, k * D:(k + 1) * D],
                       col("n1_g", k))
                last = scaled(wgate_hi[:, k, :], staged(0)[:, GT + k * D:GT + (k + 1) * D], col("n1_g", k))
            last.then_inc(prep_hi, 1)
            act.wait_ge(prep_T, 3)
            scaled(wout_hi[:, :, :].rearrange("p s d -> p (s d)"), staged(1)[:, GT:2 * GT]).then_inc(prep_hi, 1)
            for k in range(KT):
                act.wait_ge(prep_T, 4 + k)
                scaled(wup_hi[:, k, :], staged(k), col("n2_g", k)).then_inc(prep_hi, 1)
            for half in range(2):
                act.wait_ge(prep_T, 6 + half)
                scaled(wdown_hi[:, half * MT // 2:(half + 1) * MT // 2, :].rearrange("p c d -> p (c d)"),
                       staged(half)).then_inc(prep_hi, 1)

            def second_setup():
                act.wait_ge(deq_done, 1)
                for k in range(KT):
                    last = scaled(fup_hi[:, k, :], q_raw[:, k * M:(k + 1) * M], col("gamma", k))
                last.then_inc(fhi_done, 1)
                act.wait_ge(deq_done, 2)
                scaled(fdown_hi[:, :, :].rearrange("p c d -> p (c d)"), q_raw, 0.5).then_inc(fhi_done, 1)

            def norm_rows(dst, src, st, done):
                for t in range(ST):
                    last = scaled(dst[:, t, :], src[:, t, :], st.r[:, t:t + 1], st.shift[:, t:t + 1])
                last.then_inc(done, 1)

            def high(dst, done):
                scaled(dst[:, :, :].rearrange("p a n -> p (a n)"),
                       ps_aux[:, :, :].rearrange("p a n -> p (a n)")).then_inc(done, 1)

            def activate(i, s):
                k = step(i, s)
                bias = up_bias if s < PAIRS else fup_bias
                act.wait_ge(up_done, k + 1)
                if not isinstance(k, int) or k >= 1:
                    act.wait_ge(lo_done, k)
                if not isinstance(k, int) or k >= 2:
                    act.wait_ge(down_done, k - 1)
                for h in range(2):
                    m = 2 * (s % PAIRS) + h
                    nc.scalar.activation(hid[:, h, :], ps_hid[:, s % 2, h, :], ACT.Silu, bias=bias[:, m:m + 1])
                    last = nc.scalar.activation(hid_hi[:, s % 2, h, :], ps_hid[:, s % 2, h, :], ACT.Silu,
                                                bias=bias[:, m:m + 1])
                last.then_inc(act_done, 1)

            def iteration(i, par, on):
                n = i + 1
                if isinstance(i, int) and i == 0:
                    act.wait_ge(setup_bias, 1)
                for s in range(SLOTS):
                    if s in on.slots():
                        activate(i, s)
                    if s == 0 and on.ffn:
                        act.wait_ge(yT_ps, i)
                        high(yT_hi, yT_hid)
                    if s == 0 and on.front:
                        act.wait_ge(st_x.done, n + 1)
                        if not isinstance(n, int) or n >= 1:
                            act.wait_ge(x1_done, n)
                        norm_rows(xn, x_in[:, 1 - par, :, :], st_x, xn_done)
                    if s == 1 and on.front:
                        act.wait_ge(xT_ps, n + 1)
                        high(xT_hi, xT_hid)
                    if s == 2 and on.final:
                        act.wait_ge(z_shift, i - 1)
                        for t in range(ST):
                            last = scaled(zb[:, t, :], zb[:, t, :], st_z.r[:, t:t + 1], st_z.neg[:, t:t + 1])
                        last.then_inc(z_scaled, 1)
                    if s == 3 and on.front:
                        act.wait_ge(back_done, n + 1)
                        scaled(turned_hi[:, :, :].rearrange("p a n -> p (a n)"),
                               rot[:, :, :].rearrange("p a n -> p (a n)")).then_inc(turned_hid, 1)
                        act.wait_ge(gate_pre, n + 1)
                        nc.scalar.activation(gate[:, :, :], gate[:, :, :], ACT.Tanh, scale=0.5).then_inc(gate_done, 1)
                    if s == 6 and on.front:
                        act.wait_ge(st_1.done, n + 1)
                        norm_rows(x2n, x1, st_1, x2n_done)
                    if s == 7 and on.front:
                        act.wait_ge(x1T_ps, n + 1)
                        high(x1T_hi, x1T_hid)
                    if s == 7 and on.mlp:
                        act.wait_ge(st_y.done, i + 1)
                        if not isinstance(i, int) or i >= 1:
                            act.wait_ge(zb_done, i)
                        norm_rows(yn, y[par], st_y, yn_done)

            run(act, iteration, second_setup)

        @block.vector
        def _(dve):
            made = [0]

            def link(ins):
                made[0] += 1
                ins.then_inc(dve_setup, 1)
                dve.wait_ge(dve_setup, made[0])

            def staged(b):
                return ps_hid[:, b, :, :].rearrange("p a n -> p (a n)")

            def stats(st, src, n):
                if not isinstance(n, int) or n >= 1:
                    dve.wait_ge(st.done, n)
                for t in range(ST):
                    last = nc.vector.bn_stats(st.raw[:, t, :], src[:, t, :])
                last.then_inc(st.bn, 1)
                dve.wait_ge(dve_setup, 1)
                dve.wait_ge(st.bn, n + 1)
                for t in range(ST):
                    last = nc.vector.bn_aggr(st.mv[:, t, :], st.raw[:, t, :])
                last.then_inc(st.agg, 1)

            link(nc.vector.memset(decay[:], 0.0))
            dve.wait_ge(x_loaded, 16)
            stats(st_x, x_in[:, 0, :, :], 0)
            dve.wait_ge(cols_ps, 1)
            nc.vector.tensor_copy(vec_cols[:], ps_aux[:, 0, 0:NROW]).then_inc(cols_done, 1)
            dve.wait_ge(cols_done, 1)
            turns, whole, coarse, fine = (tiny[:, k:k + 1] for k in range(4))
            link(nc.vector.tensor_scalar(turns, col("frequency"), INV_TWO_PI, None, ALU.mult))
            link(nc.vector.tensor_scalar(whole, turns, ROUND_TO_INT, -ROUND_TO_INT, ALU.add, ALU.add))
            link(nc.vector.tensor_tensor(turns, turns, whole, ALU.subtract))
            link(nc.vector.tensor_scalar(coarse, turns, ROUND_TO_13_BITS, -ROUND_TO_13_BITS, ALU.add, ALU.add))
            link(nc.vector.tensor_tensor(fine, turns, coarse, ALU.subtract))
            dve.wait_ge(const_made, 9)
            dve.wait_ge(decay_tanh, 1)
            link(nc.vector.tensor_scalar(tiny[:, 6:7], tiny[:, 5:6], 0.5, 0.5, ALU.mult, ALU.add))
            link(nc.vector.tensor_scalar(decay[:], decay[:], tiny[:, 6:7], None, ALU.add))
            for q in range(GB):
                pos = cos_t[:, q * GT:(q + 1) * GT]
                if q:
                    dve.wait_ge(tables_sin, 2 * q)
                link(nc.vector.tensor_scalar(tab[0], pos, coarse, None, ALU.mult))
                link(nc.vector.tensor_scalar(tab[1], tab[0], ROUND_TO_INT, -ROUND_TO_INT, ALU.add, ALU.add))
                link(nc.vector.tensor_tensor(tab[0], tab[0], tab[1], ALU.subtract))
                link(nc.vector.scalar_tensor_tensor(out=tab[0], in0=pos, scalar=fine, in1=tab[0],
                                                    op0=ALU.mult, op1=ALU.add))
                link(nc.vector.tensor_scalar(tab[1], tab[0], ROUND_TO_INT, -ROUND_TO_INT, ALU.add, ALU.add))
                nc.vector.tensor_tensor(tab[2], tab[0], tab[1], ALU.subtract).then_inc(tables_arg, 1)
                dve.wait_ge(tables_arg, 2 * q + 1)
                link(nc.vector.tensor_scalar(tab[0], tab[0], 0.25, None, ALU.add))
                link(nc.vector.tensor_scalar(tab[1], tab[0], ROUND_TO_INT, -ROUND_TO_INT, ALU.add, ALU.add))
                nc.vector.tensor_tensor(tab[3], tab[0], tab[1], ALU.subtract).then_inc(tables_arg, 1)
            dve.wait_ge(small_in, 16 * (5 + 2 * H))

            def dot(k, src, vec):
                link(nc.vector.tensor_tensor_reduce(out=junk, in0=src, in1=vec, scale=1.0, scalar=0.0,
                                                    op0=ALU.mult, op1=ALU.add, accum_out=dots[:, k:k + 1]))

            dve.wait_ge(rows_in, 16 * 15)
            for s in range(2):
                dot(s, raw_in[:, s, :], n1_b_bc)
            for e in range(KT):
                dot(2 + e, raw_gate[:, e, :], n1_b_bc)
            a = cols["gate_b"][0]
            link(nc.vector.tensor_tensor(gate_col[:], dots[:, 2:2 + KT], vec_cols[:, a:a + KT], ALU.add))
            for e in range(KT):
                last = nc.vector.tensor_scalar(gate_fan[:, e, :], ident[:], 0.0, gate_col[:, e:e + 1],
                                               ALU.mult, ALU.add)
            last.then_inc(fan_done, 1)
            for s in range(2):
                last = nc.vector.tensor_copy(coup[:, 1, s * K:(s + 1) * K], coup[:, 0, (1 - s) * K:(2 - s) * K])
            last.then_inc(coup_done, 1)
            dve.wait_ge(prep_T, 2)
            nc.vector.tensor_scalar(outT, staged(1)[:, 0:D], 0.5, None, ALU.mult).then_inc(outT_done, 1)
            nc.vector.tensor_scalar(fc2_half[:], fc2_b_bc, 0.5, None, ALU.mult)

            def low(dst, src, scale, hi, done=None):
                last = nc.vector.scalar_tensor_tensor(out=dst, in0=src, scalar=scale, in1=hi.bitcast(F32),
                                                      op0=ALU.mult, op1=ALU.subtract)
                if done:
                    last.then_inc(done, 1)

            dve.wait_ge(prep_hi, 1)
            for k in range(KT):
                low(win_lo[:, k, :, :].rearrange("p s c -> p (s c)"), staged(0)[:, k * D:(k + 1) * D],
                    col("n1_g", k), win_hi[:, k, :, :].rearrange("p s c -> p (s c)"))
                low(wgate_lo[:, k, :], staged(0)[:, GT + k * D:GT + (k + 1) * D], col("n1_g", k),
                    wgate_hi[:, k, :], prep_lo if k == KT - 1 else None)
            dve.wait_ge(gate_bias_ps, 1)
            nc.vector.tensor_copy(gate_bias[:], ps_aux[:, 1, 0:D]).then_inc(gate_bias_made, 1)
            dve.wait_ge(prep_hi, 2)
            low(wout_lo[:, :, :].rearrange("p s d -> p (s d)"), staged(1)[:, GT:2 * GT], 1.0,
                wout_hi[:, :, :].rearrange("p s d -> p (s d)"), prep_lo)
            dve.wait_ge(w1_in, 16)
            for m in range(MT):
                dot(2 + KT + m, raw_w1[:, m, :], n2_b_bc)
            for k in range(KT):
                dve.wait_ge(prep_hi, 3 + k)
                low(wup_lo[:, k, :], staged(k), col("n2_g", k), wup_hi[:, k, :], prep_lo)
            for half in range(2):
                dve.wait_ge(prep_hi, 5 + half)
                part = slice(half * MT // 2, (half + 1) * MT // 2)
                low(wdown_lo[:, part, :].rearrange("p c d -> p (c d)"), staged(half), 1.0,
                    wdown_hi[:, part, :].rearrange("p c d -> p (c d)"), prep_lo)
            a = cols["b1"][0]
            nc.vector.tensor_tensor(up_bias[:], dots[:, 2 + KT:], vec_cols[:, a:a + MT], ALU.add).then_inc(dots_done, 1)
            dve.wait_ge(tables_sin, 2 * GB)

            def second_setup():
                def dequantise(loaded):
                    dve.wait_ge(loaded, 32)
                    nc.vector.scalar_tensor_tensor(out=q_raw, in0=q_raw.bitcast(I32), scalar=-128.0, in1=q_scale,
                                                   op0=ALU.add, op1=ALU.mult).then_inc(deq_done, 1)

                dequantise(q1_in)
                dve.wait_ge(fhi_done, 1)
                for k in range(KT):
                    low(fup_lo[:, k, :], q_raw[:, k * M:(k + 1) * M], col("gamma", k), fup_hi[:, k, :],
                        flo_done if k == KT - 1 else None)
                dve.wait_ge(fbias_ps, 1)
                b = cols["fb1"][0]
                nc.vector.tensor_tensor(fup_bias[:], ps_aux[:, 0, 0:MT], vec_cols[:, b:b + MT],
                                        ALU.add).then_inc(setup_bias, 1)
                dequantise(q2_in)
                dve.wait_ge(fhi_done, 2)
                low(fdown_lo[:, :, :].rearrange("p c d -> p (c d)"), q_raw, 0.5,
                    fdown_hi[:, :, :].rearrange("p c d -> p (c d)"), flo_done)

            def wide(buf):
                return buf.rearrange("p a n -> p (a n)")

            def low_of_aux(dst, hi, done):
                nc.vector.tensor_tensor(wide(dst[:, :, :]), wide(ps_aux[:, :, :]),
                                        wide(hi[:, :, :]).bitcast(F32), ALU.subtract).then_inc(done, 1)

            def low_of_hidden(i, s):
                k = step(i, s)
                dve.wait_ge(act_done, k + 1)
                if not isinstance(k, int) or k >= 2:
                    dve.wait_ge(down_done, k - 1)
                nc.vector.tensor_tensor(wide(hid_lo[:, s % 2, :, :]), wide(hid),
                                        wide(hid_hi[:, s % 2, :, :]).bitcast(F32),
                                        ALU.subtract).then_inc(lo_done, 1)

            def iteration(i, par, on):
                n = i + 1
                for s in range(SLOTS):
                    if s in on.slots():
                        low_of_hidden(i, s)
                    if s == 0 and on.ffn:
                        dve.wait_ge(yT_hid, i)
                        low_of_aux(yT_lo, yT_hi, yT_lod)
                    if s == 0 and on.final:
                        dve.wait_ge(down_done, step(i - 1, SLOTS - 1) + 1)
                        nc.vector.tensor_tensor(zb, ps_acc[:, :, :], zb, ALU.add).then_inc(z_done, 1)
                        dve.wait_ge(z_done, i - 1)
                        if not isinstance(i, int) or i > 2:
                            dve.wait_ge(z_scaled, i - 2)
                        stats(st_z, zb, i - 2)
                    if s == 1 and on.front:
                        dve.wait_ge(xT_hid, n + 1)
                        low_of_aux(xT_lo, xT_hi, xT_lod)
                    if s == 2 and on.front:
                        if isinstance(n, int):
                            table = slice(n % GB * GT, (n % GB + 1) * GT)
                            place = slice(n % GB, n % GB + 1)
                        else:
                            table = bass.ts(n % GB, GT)
                            place = bass.ts(n % GB, 1)
                        dve.wait_ge(beta_ps, n + 1)
                        for w, t in ((0, cos_t), (1, sin_t)):
                            last = nc.vector.scalar_tensor_tensor(
                                out=rot[:, w, :], in0=ps_aux[:, w, :], scalar=beta_bias[:, w:w + 1], in1=t[:, table],
                                op0=ALU.add, op1=ALU.mult)
                        last.then_inc(rot_done, 1)
                        dve.wait_ge(rot_done, n + 1)
                        nc.vector.tensor_tensor(rot[:, 0, :], rot[:, 0, :], rot[:, 1, :],
                                                ALU.add).then_inc(turned_in, 1)
                        if isinstance(n, int) and n == 0:
                            start = 0.0
                        else:
                            nc.vector.tensor_tensor(carry[:], scanned[:, GT - 1:GT], carry_mask[:, place],
                                                    ALU.mult).then_inc(carry_done, 1)
                            dve.wait_ge(carry_done, n)
                            start = carry[:]
                        dve.wait_ge(turned_in, n + 1)
                        nc.vector.tensor_tensor_scan(scanned[:], decay[:], rot[:, 0, :], start, ALU.mult,
                                                     ALU.add).then_inc(scan_done, 1)
                        dve.wait_ge(scan_done, n + 1)
                        for w, t in ((0, cos_t), (1, sin_t)):
                            last = nc.vector.tensor_tensor(rot[:, w, :], scanned[:], t[:, table], ALU.mult)
                        last.then_inc(back_done, 1)
                    if s == 3 and on.front:
                        dve.wait_ge(gate_ps, n + 1)
                        nc.vector.tensor_tensor(gate[:, :, :], aux_rows, over_rows(gate_bias[:]),
                                                ALU.add).then_inc(gate_pre, 1)
                        dve.wait_ge(turned_hid, n + 1)
                        nc.vector.tensor_tensor(wide(turned_lo[:, :, :]), wide(rot[:, :, :]),
                                                wide(turned_hi[:, :, :]).bitcast(F32),
                                                ALU.subtract).then_inc(turned_lod, 1)
                    if s == 4 and on.front:
                        dve.wait_ge(gate_done, n + 1)
                        dve.wait_ge(out_ps, n + 1)
                        nc.vector.scalar_tensor_tensor(out=gate[:, :, :], in0=gate[:, :, :], scalar=1.0,
                                                       in1=aux_rows, op0=ALU.add, op1=ALU.mult).then_inc(gated, 1)
                        dve.wait_ge(gated, n + 1)
                        if on.mlp:
                            dve.wait_ge(x1b_done, n)
                            dve.wait_ge(x2n_done, n)
                        for t in range(ST):
                            last = nc.vector.scalar_tensor_tensor(
                                out=x1[:, t, :], in0=xn[:, t, :], scalar=st_x.ratio[:, t:t + 1],
                                in1=gate[:, t, :], op0=ALU.mult, op1=ALU.add)
                        last.then_inc(x1_done, 1)
                    if s == 4 and on.mlp:
                        dve.wait_ge(down_done, step(i, PAIRS - 1) + 1)
                        dve.wait_ge(x1b_done, i + 1)
                        nc.vector.tensor_tensor(x1b, ps_acc[:, :, :], x1b, ALU.add).then_inc(x2_done, 1)
                    if s == 4 and on.front:
                        dve.wait_ge(x1_done, n + 1)
                        stats(st_1, x1, n)
                    if s == 4 and on.mlp:
                        dve.wait_ge(x2_done, i + 1)
                        stats(st_2, x1b, i)
                    if s == 6 and on.ffn:
                        if on.final:
                            dve.wait_ge(stored, 16 * (i - 1))
                        for t in range(ST):
                            last = nc.vector.scalar_tensor_tensor(
                                out=zb[:, t, :], in0=yn[:, t, :], scalar=st_y.ratio[:, t:t + 1],
                                in1=fc2_half[:], op0=ALU.mult, op1=ALU.add)
                        last.then_inc(zb_done, 1)
                    if s == 6 and on.mlp:
                        dve.wait_ge(st_2.done, i + 1)
                        if on.final:
                            dve.wait_ge(out_done, i - 1)
                        for t in range(ST):
                            last = nc.vector.scalar_tensor_tensor(
                                out=y[par][:, t, :], in0=x1b[:, t, :], scalar=st_2.r[:, t:t + 1],
                                in1=x_in[:, par, t, :], op0=ALU.mult, op1=ALU.add)
                        last.then_inc(y_done, 1)
                        dve.wait_ge(y_done, i + 1)
                        stats(st_y, y[par], i)
                    if s == 7 and on.front:
                        dve.wait_ge(x1T_hid, n + 1)
                        low_of_aux(x1T_lo, x1T_hi, x1T_lod)
                    if s == 7 and on.next_stat:
                        dve.wait_ge(x_loaded, 16 * (i + 3))
                        stats(st_x, x_in[:, par, :, :], i + 2)

            run(dve, iteration, second_setup)


_INS = ["L0_attn_x", "L0_attn_in_proj_w", "L0_attn_log_decay", "L0_attn_frequency", "L0_attn_coupling",
        "L0_attn_out_proj_w", "L0_attn_gate_w", "L0_attn_gate_b", "L0_attn_n1_g", "L0_attn_n1_b",
        "L0_attn_n2_g", "L0_attn_n2_b", "L0_attn_mlp_w1", "L0_attn_mlp_b1", "L0_attn_mlp_w2", "L0_attn_mlp_b2",
        "L0_ffn_ln_gamma", "L0_ffn_ln_beta", "L0_ffn_fc1_q", "L0_ffn_fc1_scales", "L0_ffn_fc1_bias",
        "L0_ffn_fc2_q", "L0_ffn_fc2_scales", "L0_ffn_fc2_bias"]


def kernel(**inputs):
    import numpy as np
    import concourse.bacc as bacc
    from concourse.bass_utils import run_bass_kernel_spmd

    nc = bacc.Bacc("TRN2", target_bir_lowering=False, num_devices=1)
    arrays, args = {}, []
    for name in _INS:
        a = np.ascontiguousarray(inputs[name])
        arrays[f"in_{name}"] = a
        args.append(nc.dram_tensor(f"in_{name}", a.shape, mybir.dt.from_np(a.dtype), kind="ExternalInput").ap())
    shape = arrays["in_L0_attn_x"].shape
    out = nc.dram_tensor("out", shape, F32, kind="ExternalOutput").ap()
    build(nc, *args, out)
    r = run_bass_kernel_spmd(nc, [arrays], core_ids=[0])
    return r.results[0]["out"]
```

```python
from contextlib import ExitStack

import concourse.bass as bass
from concourse import mybir

F32 = mybir.dt.float32
F32R = mybir.dt.float32r
I32 = mybir.dt.int32
ALU = mybir.AluOpType
ACT = mybir.ActivationFunctionType

P = 128
EPS = 1e-5
ROUND_TO_INT = 12582912.0
ROUND_TO_13_BITS = 1536.0
INV_TWO_PI = 0.15915494309189535
TURN = 6.283185


def build(nc, x, in_proj_w, log_decay, frequency, coupling, out_proj_w, gate_w, gate_b, n1_g, n1_b,
          n2_g, n2_b, mlp_w1, mlp_b1, mlp_w2, mlp_b2, ln_gamma, ln_beta, fc1_q, fc1_scales, fc1_bias,
          fc2_q, fc2_scales, fc2_bias, out):
    B, T, D = x.shape
    K2 = in_proj_w.shape[0]
    K = K2 // 2
    H, KH, _ = coupling.shape
    M = mlp_w1.shape[0]
    KT = D // P
    MT = M // P
    PAIRS = MT // 2
    GT = 512
    ST = GT // P
    G = B * T // GT
    GB = T // GT
    SLOTS = 2 * PAIRS
    assert K2 == P and GT == 512 and D == 256 and fc1_q.shape == (D, M) and fc1_scales.shape[0] == KT
    assert GB == 4 and G == 16

    x_rows = x.rearrange("b (g t p) d -> (b g) p t d", t=ST, p=P)
    out_rows = out.rearrange("b (g t p) d -> (b g) p t d", t=ST, p=P)

    with ExitStack() as ctx:
        def sb(name, shape, dt=F32):
            return ctx.enter_context(nc.sbuf_tensor(name, shape, dt))

        def sem(name):
            return ctx.enter_context(nc.semaphore(name))

        win_hi, win_lo = (sb(f"win_{h}", [P, KT, P], F32R) for h in ("hi", "lo"))
        wgate_hi, wgate_lo = (sb(f"wgate_{h}", [P, KT, D], F32R) for h in ("hi", "lo"))
        wout_hi, wout_lo = (sb(f"wout_{h}", [P, D], F32R) for h in ("hi", "lo"))
        wup_hi, wup_lo = (sb(f"wup_{h}", [P, KT, M], F32R) for h in ("hi", "lo"))
        wdown_hi, wdown_lo = (sb(f"wdown_{h}", [P, MT, D], F32R) for h in ("hi", "lo"))
        fup_hi, fup_lo = (sb(f"fup_{h}", [P, KT, M], F32R) for h in ("hi", "lo"))
        fdown_hi, fdown_lo = (sb(f"fdown_{h}", [P, MT, D], F32R) for h in ("hi", "lo"))

        ident = sb("ident", [P, P])
        cos_t = sb("cos_t", [P, T])
        sin_t = sb("sin_t", [P, T])
        decay = sb("decay", [P, GT])
        gate_bias = sb("gate_bias", [P, D])
        vec_bc = sb("vec_bc", [P, 4, D])
        n1_b_bc, n2_b_bc, mlp_b2_bc, fc2_b_bc = (vec_bc[:, k, :] for k in range(4))
        coup = sb("coup", [P, P])
        carry_mask = sb("carry_mask", [P, GB])
        half_power = sb("half_power", [P, 3, ST])
        NROW = 4 * KT + 2 * MT + KT + 2
        vec_rows = sb("vec_rows", [32, P])
        vec_cols = sb("vec_cols", [P, NROW])
        r0 = 0
        cols = {}
        for name, n in (("n1_g", KT), ("n2_g", KT), ("gamma", KT), ("beta", KT), ("b1", MT), ("fb1", MT),
                        ("gate_b", KT), ("log_decay", 1), ("frequency", 1)):
            cols[name] = (r0, n)
            r0 += n

        def col(name, k=0):
            return vec_cols[:, cols[name][0] + k:cols[name][0] + k + 1]

        eps_tile = sb("eps_tile", [P, ST])
        dots = sb("dots", [P, 1 + KT + MT])
        beta_bias = dots[:, 0:1]
        gate_col = sb("gate_col", [P, KT])
        up_bias = sb("up_bias", [P, MT])
        fup_bias = sb("fup_bias", [P, MT])
        tiny = sb("tiny", [P, 8])
        fc2_half = sb("fc2_half", [P, D])

        x_in = sb("x_in", [P, 2, ST, D])
        xn = sb("xn", [P, ST, D])
        xT_hi, xT_lo = (sb(f"xT_{h}", [P, KT, GT], F32R) for h in ("hi", "lo"))
        rot = sb("rot", [P, 2, GT])
        scanned = sb("scanned", [P, GT])
        turned_hi, turned_lo = (sb(f"turned_{h}", [P, GT], F32R) for h in ("hi", "lo"))
        gate = sb("gate", [P, ST, D])
        mid = sb("mid", [P, 4, ST * D])
        x1, x1b, x2n = (mid[:, k, :].rearrange("p (t d) -> p t d", d=D) for k in range(3))
        hid = mid[:, 3, :].rearrange("p (m n) -> p m n", n=GT)
        x1T_hi, x1T_lo = (sb(f"x1T_{h}", [P, KT, GT], F32R) for h in ("hi", "lo"))
        hid_hi, hid_lo = (sb(f"hid_{h}", [P, 2, 2, GT], F32R) for h in ("hi", "lo"))
        late = sb("late", [P, 4, ST * D])
        y = [late[:, k, :].rearrange("p (t d) -> p t d", d=D) for k in range(2)]
        yn, zb = (late[:, k, :].rearrange("p (t d) -> p t d", d=D) for k in (2, 3))
        yT_hi, yT_lo = (sb(f"yT_{h}", [P, KT, GT], F32R) for h in ("hi", "lo"))
        carry = sb("carry", [P, 1])

        y_shift = [sb(f"y_shift{k}", [P, ST]) for k in range(2)]

        class Stat:
            def __init__(self, name, double):
                self.raw = sb(f"{name}_raw", [P, ST, 6])
                self.mv = sb(f"{name}_mv", [P, ST, 2])
                self.var = sb(f"{name}_var", [P, 3, ST])
                self.pow = sb(f"{name}_pow", [P, 3, ST])
                self.neg = sb(f"{name}_neg", [P, ST])
                self.shift = sb(f"{name}_shift", [P, ST])
                self.ratio = sb(f"{name}_ratio", [P, ST])
                self.double = double
                self.bn = sem(f"{name}_bn")
                self.agg = sem(f"{name}_agg")
                self.eps = sem(f"{name}_eps")
                self.powd = sem(f"{name}_powd")
                self.done = sem(f"{name}_done")
                self.r = self.pow[:, 1 if double else 0, :]

        st_x, st_1, st_2, st_y, st_z = (Stat(n, d) for n, d in
                                        (("sx", True), ("s1", False), ("s2", False), ("sy", True), ("sz", False)))

        raw_w1 = mid[:, 0:2, :].rearrange("p a (c d) -> p (a c) d", d=D)
        raw_w2 = mid[:, 2:4, :]
        flat = late[:, :, :].rearrange("p a b -> p (a b)")
        raw_in = flat[:, 0:D]
        raw_gate = flat[:, 2 * D:2 * D + KT * D].rearrange("p (e d) -> p e d", d=D)
        raw_out = flat[:, 4 * D:5 * D].rearrange("p (e k) -> p e k", k=P)
        outT = flat[:, 5 * D:6 * D]
        junk = rot[:, 1, 0:D]
        gate_fan = flat[:, 7 * D:8 * D].rearrange("p (e q) -> p e q", q=P)
        TAB = GT + GB
        tab = [flat[:, 8 * D + k * TAB:8 * D + (k + 1) * TAB] for k in range(3)]
        starts = sb("starts", [P, 2, GB])
        q_raw = late[:, 0:2, :].rearrange("p a b -> p (a b)")
        q_scale = late[:, 2:4, :].rearrange("p a b -> p (a b)")

        ps_hid = ctx.enter_context(nc.psum_tensor("ps_hid", [P, 2, 2, GT], F32))
        ps_acc = ctx.enter_context(nc.psum_tensor("ps_acc", [P, ST, D], F32))
        ps_aux = ctx.enter_context(nc.psum_tensor("ps_aux", [P, 2, GT], F32))
        aux_rows = ps_aux[:, :, :].rearrange("p a (s d) -> p (a s) d", d=D)

        rows_in = sem("rows_in")
        bc_in = sem("bc_in")
        small_in = sem("small_in")
        coup_zero = sem("coup_zero")
        w1_in, w2_in = sem("w1_in"), sem("w2_in")
        q1_in, q2_in = sem("q1_in"), sem("q2_in")
        x_loaded = sem("x_loaded")
        stored = sem("stored")
        const_made = sem("const_made")
        ident_zero = sem("ident_zero")
        dve_setup = sem("dve_setup")
        cols_ps, cols_done = sem("cols_ps"), sem("cols_done")
        prep_T = sem("prep_T")
        prep_hi = sem("prep_hi")
        prep_lo = sem("prep_lo")
        outT_done = sem("outT_done")
        fan_done = sem("fan_done")
        dots_done = sem("dots_done")
        gate_bias_made = sem("gate_bias_made")
        gate_bias_ps = sem("gate_bias_ps")
        tables_arg = sem("tables_arg")
        tables_sin = sem("tables_sin")
        starts_done = sem("starts_done")
        decay_tanh = sem("decay_tanh")
        deq_done = sem("deq_done")
        fhi_done = sem("fhi_done")
        flo_done = sem("flo_done")
        fbias_ps = sem("fbias_ps")
        setup_bias = sem("setup_bias")

        xn_done = sem("xn_done")
        xT_ps = sem("xT_ps")
        xT_hid, xT_lod = sem("xT_hid"), sem("xT_lod")
        beta_ps = sem("beta_ps")
        rot_done = sem("rot_done")
        turned_in = sem("turned_in")
        back_parts = sem("back_parts")
        scan_done = sem("scan_done")
        carry_done = sem("carry_done")
        back_done = sem("back_done")
        turned_hid, turned_lod = sem("turned_hid"), sem("turned_lod")
        gate_ps = sem("gate_ps")
        gate_pre = sem("gate_pre")
        gate_done = sem("gate_done")
        out_ps = sem("out_ps")
        gated = sem("gated")
        x1_done = sem("x1_done")
        x1b_done = sem("x1b_done")
        x2n_done = sem("x2n_done")
        x1T_ps = sem("x1T_ps")
        x1T_hid, x1T_lod = sem("x1T_hid"), sem("x1T_lod")
        up_done = sem("up_done")
        act_done = sem("act_done")
        lo_done = sem("lo_done")
        down_done = sem("down_done")
        x2_done = sem("x2_done")
        y_done = sem("y_done")
        yn_done = sem("yn_done")
        yT_ps = sem("yT_ps")
        yT_hid, yT_lod = sem("yT_hid"), sem("yT_lod")
        zb_done = sem("zb_done")
        z_done = sem("z_done")
        z_shift = sem("z_shift")
        y_shift_done = sem("y_shift_done")
        z_scaled = sem("z_scaled")
        out_done = sem("out_done")

        def step(i, s):
            if isinstance(i, int) and (i == 0 or i == G):
                return s if i == 0 else SLOTS * G - 2 * PAIRS + s
            return i * SLOTS + (s - PAIRS)

        def over_rows(vec):
            return vec.unsqueeze(1).to_broadcast([P, ST, D])

        class Stages:
            def __init__(self, front=True, mlp=True, ffn=True, final=True, next_stat=True,
                         turn=1, beta=2, gate=3, out=4, norm=6, turn2=7, close=2):
                self.front, self.mlp, self.ffn, self.final, self.next_stat = front, mlp, ffn, final, next_stat
                self.turn, self.beta, self.gate, self.out = turn, beta, gate, out
                self.norm, self.turn2, self.close = norm, turn2, close

            def slots(self):
                return [s for s in range(SLOTS) if (self.mlp if s < PAIRS else self.ffn)]

        def stages(i):
            on = dict(front=i + 1 < G, mlp=0 <= i < G, ffn=1 <= i <= G, final=2 <= i, next_stat=i + 2 < G)
            if i == 0:
                on.update(turn=0, beta=1, gate=2, out=3, norm=4, turn2=5)
            if i == G:
                on.update(close=PAIRS)
            return Stages(**on)

        LOOP_FROM, LOOP_TO = 2, G - 2

        def run(eng, iteration):
            for i in range(-1, LOOP_FROM):
                iteration(i, i % 2, stages(i))
            with eng.Fori(0, (LOOP_TO - LOOP_FROM) // 2) as j:
                for u in range(2):
                    iteration(j * 2 + (LOOP_FROM + u), u, Stages())
            for i in range(LOOP_TO, G + 2):
                iteration(i, i % 2, stages(i))

        block = ctx.enter_context(nc.Block())

        @block.sync
        def _(sp):
            def load_x(n, par):
                sp.dma_start(x_in[:, par, :, :], x_rows[n]).then_inc(x_loaded, 16)

            def rows(name, vec):
                a, n = cols[name]
                sp.dma_start(vec_rows[a:a + n, :], vec.rearrange("(k p) -> k p", p=P)).then_inc(rows_in, 16)

            load_x(0, 0)
            for name, vec in (("log_decay", log_decay), ("frequency", frequency)):
                a = cols[name][0]
                for half in range(2):
                    sp.dma_start(vec_rows[a:a + 1, half * K:(half + 1) * K],
                                 vec.rearrange("(a k) -> a k", a=1)).then_inc(rows_in, 16)
            for name, vec in (("n1_g", n1_g), ("n2_g", n2_g), ("gamma", ln_gamma), ("beta", ln_beta),
                              ("b1", mlp_b1), ("fb1", fc1_bias), ("gate_b", gate_b)):
                rows(name, vec)
            for k, vec in enumerate((n1_b, n2_b, mlp_b2, fc2_bias)):
                sp.dma_start(vec_bc[:, k, :], vec.partition_broadcast(P)).then_inc(bc_in, 16)
            sp.dma_start(raw_w1, mlp_w1.rearrange("(c p) d -> p c d", p=P)).then_inc(w1_in, 16)
            sp.dma_start(raw_w2, mlp_w2.rearrange("(e p) m -> p e m", p=P)).then_inc(w2_in, 16)
            sp.wait_ge(st_x.agg, 1)
            load_x(1, 1)
            sp.wait_ge(prep_T, 3)
            sp.wait_ge(gate_bias_ps, 1)
            sp.wait_ge(dots_done, 1)
            sp.wait_ge(tables_sin, 2)
            sp.dma_start(q_raw.bitcast(I32).rearrange("p (k m) -> p k m", m=M),
                         fc1_q.rearrange("(k p) m -> p k m", p=P)).then_inc(q1_in, 16)
            sp.dma_start(q_scale.rearrange("p (k m) -> p k m", m=M),
                         fc1_scales.partition_broadcast(P)).then_inc(q1_in, 16)
            sp.wait_ge(flo_done, 1)
            sp.wait_ge(fbias_ps, 1)
            sp.dma_start(q_raw.bitcast(I32).rearrange("p (c d) -> p c d", d=D),
                         fc2_q.rearrange("(c p) d -> p c d", p=P)).then_inc(q2_in, 16)
            sp.dma_start(q_scale.rearrange("p (c d) -> p c d", d=D),
                         fc2_scales.partition_broadcast(P)).then_inc(q2_in, 16)

            def iteration(i, par, on):
                if on.final:
                    sp.wait_ge(out_done, i - 1)
                    sp.dma_start(out_rows[i - 2], zb).then_inc(stored, 16)
                if on.mlp and on.next_stat:
                    sp.wait_ge(y_done, i + 1)
                    sp.dma_start(x_in[:, par, :, :], x_rows[i + 2]).then_inc(x_loaded, 16)

            run(sp, iteration)
            sp.wait_ge(stored, 16 * G)

        @block.gpsimd
        def _(pool):
            nc.gpsimd.memset(coup[:], 0.0).then_inc(coup_zero, 1)
            nc.gpsimd.memset(ident[:], 0.0).then_inc(ident_zero, 1)
            pool.wait_ge(ident_zero, 1)
            nc.gpsimd.affine_select(out=ident[:], in_=ident[:], compare_op=ALU.not_equal, fill=1.0, base=0,
                                    pattern=[[-1, P]], channel_multiplier=1).then_inc(const_made, 1)
            nc.gpsimd.memset(eps_tile[:], EPS).then_inc(const_made, 1)
            nc.gpsimd.memset(half_power[:, 0:2, :], -0.5).then_inc(const_made, 1)
            nc.gpsimd.memset(half_power[:, 2:3, :], 0.5).then_inc(const_made, 1)
            nc.gpsimd.memset(carry_mask[:, 0:1], 0.0).then_inc(const_made, 1)
            nc.gpsimd.memset(carry_mask[:, 1:GB], 1.0).then_inc(const_made, 1)
            nc.gpsimd.memset(tiny[:, 4:5], -TURN).then_inc(const_made, 1)
            nc.gpsimd.iota(cos_t[:, 0:GT], pattern=[[1, GT]], base=0, channel_multiplier=0,
                           allow_small_or_imprecise_dtypes=True).then_inc(const_made, 1)
            nc.gpsimd.iota(cos_t[:, GT:TAB], pattern=[[GT, GB]], base=0, channel_multiplier=0,
                           allow_small_or_imprecise_dtypes=True).then_inc(const_made, 1)
            pool.wait_ge(const_made, 9)
            nc.gpsimd.memset(tiny[K:K2, 4:5], TURN).then_inc(const_made, 1)
            pool.wait_ge(const_made, 10)

            def stat(st, n, free):
                pool.wait_ge(st.agg, n + 1)
                free()
                last = nc.gpsimd.tensor_tensor(st.var[:, 0, :], st.mv[:, :, 1], eps_tile[:, :], ALU.add)
                if st.double:
                    for k in (1, 2):
                        last = nc.gpsimd.tensor_scalar(st.var[:, k, :], st.mv[:, :, 1], 1.0 + EPS, EPS * EPS,
                                                       ALU.mult, ALU.add)
                last.then_inc(st.eps, 1)
                nc.gpsimd.tensor_scalar(st.neg[:, :], st.mv[:, :, 0], -1.0, 0.0, ALU.mult, ALU.add)
                k = 3 if st.double else 1
                pool.wait_ge(st.eps, n + 1)
                nc.gpsimd.tensor_tensor(st.pow[:, 0:k, :], st.var[:, 0:k, :], half_power[:, 0:k, :],
                                        ALU.pow).then_inc(st.powd, 1)
                pool.wait_ge(st.powd, n + 1)
                if st.double:
                    nc.gpsimd.tensor_tensor(st.ratio[:, :], st.pow[:, 0, :], st.pow[:, 2, :], ALU.mult)
                nc.gpsimd.tensor_tensor(st.shift[:, :], st.neg[:, :], st.r, ALU.mult).then_inc(st.done, 1)

            def free_x(n):
                def f():
                    if not isinstance(n, int) or n > 0:
                        pool.wait_ge(xn_done, n)
                        pool.wait_ge(x1_done, n)
                return f

            stat(st_x, 0, free_x(0))

            def iteration(i, par, on):
                if on.final:
                    def free_z():
                        if not isinstance(i, int) or i > 2:
                            pool.wait_ge(z_scaled, i - 2)
                    stat(st_z, i - 2, free_z)
                    pool.wait_ge(y_shift_done, i - 1)
                    pool.wait_ge(st_z.done, i - 1)
                    nc.gpsimd.tensor_tensor(st_z.neg[:, :], st_z.shift[:, :], y_shift[par][:, :],
                                            ALU.add).then_inc(z_shift, 1)
                    pool.wait_ge(z_scaled, i - 1)
                    nc.gpsimd.tensor_tensor(zb, zb, y[par], ALU.add).then_inc(out_done, 1)
                if on.front:
                    def free_1():
                        if not isinstance(i, int) or i >= 0:
                            pool.wait_ge(x2n_done, i + 1)
                    stat(st_1, i + 1, free_1)
                if on.mlp:
                    def free_2():
                        if not isinstance(i, int) or i > 0:
                            pool.wait_ge(y_done, i)
                    stat(st_2, i, free_2)
                    nc.gpsimd.tensor_tensor(y_shift[par][:, :], st_2.neg[:, :], st_2.r, ALU.mult).then_inc(
                        y_shift_done, 1)

                    def free_y():
                        if not isinstance(i, int) or i > 0:
                            pool.wait_ge(yn_done, i)
                            pool.wait_ge(zb_done, i)
                    stat(st_y, i, free_y)
                if on.front:
                    pool.wait_ge(x1_done, i + 2)
                    if on.mlp:
                        pool.wait_ge(y_done, i + 1)
                    nc.gpsimd.tensor_tensor(x1b, x1, over_rows(mlp_b2_bc), ALU.add).then_inc(x1b_done, 1)
                if on.next_stat:
                    stat(st_x, i + 2, free_x(i + 2))

            run(pool, iteration)


        @block.tensor
        def _(pe):
            def transpose(dst, src):
                k = src.partition_size()
                return nc.tensor.transpose(dst, src, ident[0:k, 0:k])

            def staged(b):
                return ps_hid[:, b, :, :].rearrange("p a n -> p (a n)")

            pe.wait_ge(const_made, 10)
            pe.wait_ge(rows_in, 16 * 11)
            transpose(ps_aux[:, 0, 0:NROW], vec_rows[0:NROW, :]).then_inc(cols_ps, 1)
            pe.wait_ge(small_in, 16 * (3 + 2 * H))
            for k in range(KT):
                transpose(staged(0)[:, k * P:(k + 1) * P], raw_in[:, k * P:(k + 1) * P])
            for k in range(KT):
                for e in range(KT):
                    last = transpose(staged(0)[:, GT + (2 * k + e) * P:GT + (2 * k + e + 1) * P],
                                     raw_gate[:, e, k * P:(k + 1) * P])
            last.then_inc(prep_T, 1)
            for e in range(KT):
                last = transpose(staged(1)[:, e * P:(e + 1) * P], raw_out[:, e, :])
            last.then_inc(prep_T, 1)
            pe.wait_ge(fan_done, 1)
            for e in range(KT):
                last = nc.tensor.matmul(ps_aux[:, 1, e * P:(e + 1) * P], gate_fan[:, e, :], ident[:],
                                        start=True, stop=True)
            last.then_inc(gate_bias_ps, 1)
            pe.wait_ge(outT_done, 1)
            nc.tensor.matmul(staged(1)[:, GT:GT + D], coup[:], outT, start=True, stop=True).then_inc(prep_T, 1)

            def turn_up_weights(k):
                pe.wait_ge(w1_in, 16)
                pe.wait_ge(prep_hi, k + 1)
                pe.wait_ge(prep_lo, k + 1)
                for c in range(MT):
                    last = transpose(staged(k)[:, c * P:(c + 1) * P], raw_w1[:, c, k * P:(k + 1) * P])
                last.then_inc(prep_T, 1)

            def turn_down_weights(half):
                pe.wait_ge(w2_in, 16)
                pe.wait_ge(prep_hi, half + 3)
                pe.wait_ge(prep_lo, half + 3)
                for c in range(MT // 2):
                    for e in range(KT):
                        a = e * M + (half * MT // 2 + c) * P
                        last = transpose(staged(half)[:, (KT * c + e) * P:(KT * c + e + 1) * P],
                                         raw_w2.rearrange("p a b -> p (a b)")[:, a:a + P])
                last.then_inc(prep_T, 1)

            def ffn_bias():
                pe.wait_ge(deq_done, 1)
                pe.wait_ge(x1T_hid, 1)
                pe.wait_ge(x1T_lod, 1)
                for m in range(MT):
                    for k in range(KT):
                        last = nc.tensor.matmul(ps_aux[:, 0, m:m + 1], q_raw[:, k * M + m * P:k * M + (m + 1) * P],
                                                col("beta", k), start=(k == 0), stop=(k == KT - 1))
                last.then_inc(fbias_ps, 1)

            def turn_rows(src, done):
                for k in range(KT):
                    for t in range(ST):
                        last = transpose(ps_aux[:, k, t * P:(t + 1) * P], src[:, t, k * P:(k + 1) * P])
                last.then_inc(done, 1)

            def three(dst, w_hi, w_lo, a_hi, a_lo, start, stop, **kw):
                nc.tensor.matmul(dst, w_hi, a_hi, start=start, stop=False, **kw)
                nc.tensor.matmul(dst, w_hi, a_lo, start=False, stop=False, **kw)
                return nc.tensor.matmul(dst, w_lo, a_hi, start=False, stop=stop, **kw)

            def rows_product(dst, t, a_hi, a_lo, w_hi, w_lo, first, final):
                return three(dst[:, t, :], a_hi, a_lo, w_hi, w_lo, start=first and t % 2 == 0, stop=final,
                             skip_group_check=True)

            def up(i, s):
                k = step(i, s)
                w_hi, w_lo, a_hi, a_lo = (wup_hi, wup_lo, x1T_hi, x1T_lo) if s < PAIRS else (fup_hi, fup_lo, yT_hi, yT_lo)
                if s == 0:
                    pe.wait_ge(x1T_hid, i + 1)
                    pe.wait_ge(x1T_lod, i + 1)
                    if isinstance(i, int) and i == 0:
                        pe.wait_ge(prep_hi, 6)
                        pe.wait_ge(prep_lo, 6)
                if s == PAIRS:
                    pe.wait_ge(yT_hid, i)
                    pe.wait_ge(yT_lod, i)
                    if isinstance(i, int) and i == 1:
                        pe.wait_ge(flo_done, 2)
                if not isinstance(k, int) or k >= 2:
                    pe.wait_ge(act_done, k - 1)
                for h in range(2):
                    m = 2 * (s % PAIRS) + h
                    for c in range(KT):
                        last = three(ps_hid[:, s % 2, h, :], w_hi[:, c, m * P:(m + 1) * P],
                                     w_lo[:, c, m * P:(m + 1) * P], a_hi[:, c, :], a_lo[:, c, :],
                                     start=(c == 0), stop=(c == KT - 1))
                last.then_inc(up_done, 1)

            def down(i, s):
                k = step(i, s)
                w_hi, w_lo = (wdown_hi, wdown_lo) if s < PAIRS else (fdown_hi, fdown_lo)
                first, final = s % PAIRS == 0, s % PAIRS == PAIRS - 1
                if s == 0 and (not isinstance(i, int) or i >= 2):
                    pe.wait_ge(z_done, i - 1)
                if s == PAIRS:
                    if isinstance(i, int) and i == G:
                        pe.wait_ge(z_done, i - 1)
                    else:
                        pe.wait_ge(x2_done, i + 1)
                pe.wait_ge(act_done, k + 1)
                pe.wait_ge(lo_done, k + 1)
                for h in range(2):
                    m = 2 * (s % PAIRS) + h
                    for t in range(ST):
                        tile = slice(t * P, (t + 1) * P)
                        last = rows_product(ps_acc, t, hid_hi[:, s % 2, h, tile], hid_lo[:, s % 2, h, tile],
                                            w_hi[:, m, :], w_lo[:, m, :], first and h == 0, final and h == 1)
                last.then_inc(down_done, 1)

            def iteration(i, par, on):
                n = i + 1
                first = isinstance(i, int) and i == -1
                for s in range(SLOTS):
                    if s in on.slots():
                        up(i, s)
                    if s == 0 and on.ffn:
                        pe.wait_ge(yn_done, i)
                        turn_rows(yn, yT_ps)
                    if s == on.turn and on.front:
                        if on.ffn:
                            pe.wait_ge(yT_hid, i)
                            pe.wait_ge(yT_lod, i)
                        if first:
                            pe.wait_ge(gate_bias_made, 1)
                        if isinstance(i, int) and i == 0:
                            pe.wait_ge(setup_bias, 1)
                        pe.wait_ge(xn_done, n + 1)
                        turn_rows(xn, xT_ps)
                        if first:
                            turn_up_weights(0)
                    if s == on.beta and on.front:
                        pe.wait_ge(xT_hid, n + 1)
                        pe.wait_ge(xT_lod, n + 1)
                        for c in range(KT):
                            last = three(ps_aux[:, 0, :], win_hi[:, c, :], win_lo[:, c, :],
                                         xT_hi[:, c, :], xT_lo[:, c, :], start=(c == 0), stop=(c == KT - 1))
                        last.then_inc(beta_ps, 1)
                        if first:
                            turn_up_weights(1)
                    if s == on.gate and on.front:
                        pe.wait_ge(rot_done, n + 1)
                        for c in range(KT):
                            for t in range(ST):
                                tile = slice(t * P, (t + 1) * P)
                                last = rows_product(aux_rows, t, xT_hi[:, c, tile], xT_lo[:, c, tile],
                                                    wgate_hi[:, c, :], wgate_lo[:, c, :], c == 0, c == KT - 1)
                        last.then_inc(gate_ps, 1)
                        if first:
                            turn_down_weights(0)
                    if s == on.out and on.front:
                        pe.wait_ge(gate_pre, n + 1)
                        pe.wait_ge(turned_hid, n + 1)
                        pe.wait_ge(turned_lod, n + 1)
                        for t in range(ST):
                            tile = slice(t * P, (t + 1) * P)
                            last = rows_product(aux_rows, t, turned_hi[:, tile], turned_lo[:, tile],
                                                wout_hi[:, :], wout_lo[:, :], True, True)
                        last.then_inc(out_ps, 1)
                        if first:
                            turn_down_weights(1)
                    if s == on.turn2 and on.front:
                        pe.wait_ge(x2n_done, n + 1)
                        pe.wait_ge(gated, n + 1)
                        turn_rows(x2n, x1T_ps)
                        if first:
                            ffn_bias()
                    if s == 0 and on.final:
                        down(i - 1, SLOTS - 1)
                    elif s > 0 and s - 1 in on.slots():
                        down(i, s - 1)

            run(pe, iteration)

        @block.scalar
        def _(act):
            def scaled(dst, src, scale=1.0, bias=0.0):
                return nc.scalar.activation(dst, src, ACT.Identity, scale=scale, bias=bias)

            def staged(b):
                return ps_hid[:, b, :, :].rearrange("p a n -> p (a n)")

            act.dma_start(raw_in, in_proj_w).then_inc(small_in, 16)
            act.dma_start(raw_gate, gate_w.rearrange("(e p) d -> p e d", p=P)).then_inc(small_in, 16)
            act.dma_start(raw_out, out_proj_w.rearrange("(e p) k -> p e k", p=P)).then_inc(small_in, 16)
            act.wait_ge(coup_zero, 1)
            for part in range(2):
                for h in range(H):
                    a = part * K + h * KH
                    act.dma_start(coup[a:a + KH, a:a + KH], coupling[h]).then_inc(small_in, 16)
            act.wait_ge(cols_done, 1)
            nc.scalar.activation(tiny[:, 7:8], col("log_decay"), ACT.Silu)
            nc.scalar.activation(tiny[:, 5:6], col("log_decay"), ACT.Tanh, scale=0.5).then_inc(decay_tanh, 1)
            act.wait_ge(prep_T, 1)
            for k in range(KT):
                scaled(win_hi[:, k, :], staged(0)[:, k * P:(k + 1) * P], col("n1_g", k))
                last = scaled(wgate_hi[:, k, :], staged(0)[:, GT + k * D:GT + (k + 1) * D], col("n1_g", k))
            last.then_inc(prep_hi, 1)
            act.wait_ge(const_made, 10)
            act.wait_ge(tables_arg, 1)
            nc.scalar.activation(sin_t[:, 0:TAB], tab[2], ACT.Sin, scale=tiny[:, 4:5]).then_inc(tables_sin, 1)
            act.wait_ge(tables_arg, 2)
            nc.scalar.activation(cos_t[:, 0:TAB], tab[0], ACT.Sin, scale=TURN).then_inc(tables_sin, 1)

            def out_weights():
                act.wait_ge(prep_T, 3)
                scaled(wout_hi[:, :], staged(1)[:, GT:GT + D]).then_inc(prep_hi, 1)

            def up_weights(k):
                act.wait_ge(prep_T, 4 + k)
                scaled(wup_hi[:, k, :], staged(k), col("n2_g", k)).then_inc(prep_hi, 1)

            def down_weights(half):
                act.wait_ge(prep_T, 6 + half)
                scaled(wdown_hi[:, half * MT // 2:(half + 1) * MT // 2, :].rearrange("p c d -> p (c d)"),
                       staged(half)).then_inc(prep_hi, 1)

            def ffn_up_weights():
                act.wait_ge(deq_done, 1)
                for k in range(KT):
                    last = scaled(fup_hi[:, k, :], q_raw[:, k * M:(k + 1) * M], col("gamma", k))
                last.then_inc(fhi_done, 1)

            def ffn_down_weights():
                act.wait_ge(deq_done, 2)
                scaled(fdown_hi[:, :, :].rearrange("p c d -> p (c d)"), q_raw, 0.5).then_inc(fhi_done, 1)

            def norm_rows(dst, src, st, done):
                for t in range(ST):
                    last = scaled(dst[:, t, :], src[:, t, :], st.r[:, t:t + 1], st.shift[:, t:t + 1])
                last.then_inc(done, 1)

            def high(dst, done):
                scaled(dst[:, :, :].rearrange("p a n -> p (a n)"),
                       ps_aux[:, :, :].rearrange("p a n -> p (a n)")).then_inc(done, 1)

            def activate(i, s):
                k = step(i, s)
                bias = up_bias if s < PAIRS else fup_bias
                act.wait_ge(up_done, k + 1)
                if not isinstance(k, int) or k >= 1:
                    act.wait_ge(lo_done, k)
                if not isinstance(k, int) or k >= 2:
                    act.wait_ge(down_done, k - 1)
                for h in range(2):
                    m = 2 * (s % PAIRS) + h
                    nc.scalar.activation(hid[:, h, :], ps_hid[:, s % 2, h, :], ACT.Silu, bias=bias[:, m:m + 1])
                    last = nc.scalar.activation(hid_hi[:, s % 2, h, :], ps_hid[:, s % 2, h, :], ACT.Silu,
                                                bias=bias[:, m:m + 1])
                last.then_inc(act_done, 1)

            def iteration(i, par, on):
                n = i + 1
                first = isinstance(i, int) and i == -1
                second = isinstance(i, int) and i == 0

                def norm_x():
                    act.wait_ge(st_x.done, n + 1)
                    if not isinstance(n, int) or n >= 1:
                        act.wait_ge(x1_done, n)
                    norm_rows(xn, x_in[:, 1 - par, :, :], st_x, xn_done)

                if second:
                    norm_x()
                    act.wait_ge(setup_bias, 1)
                for s in range(SLOTS):
                    if s == on.turn2 and on.front:
                        act.wait_ge(x1T_ps, n + 1)
                        high(x1T_hi, x1T_hid)
                    if s in on.slots():
                        activate(i, s)
                    if s == 0 and on.ffn:
                        act.wait_ge(yT_ps, i)
                        high(yT_hi, yT_hid)
                    if s == 0 and on.front and not second:
                        norm_x()
                        if first:
                            out_weights()
                    if s == on.turn and on.front:
                        act.wait_ge(xT_ps, n + 1)
                        high(xT_hi, xT_hid)
                        if first:
                            up_weights(0)
                    if s == on.close and on.final:
                        act.wait_ge(z_shift, i - 1)
                        for t in range(ST):
                            last = scaled(zb[:, t, :], zb[:, t, :], st_z.r[:, t:t + 1], st_z.neg[:, t:t + 1])
                        last.then_inc(z_scaled, 1)
                    if s == on.gate and on.front:
                        if first:
                            up_weights(1)
                        act.wait_ge(back_done, n + 1)
                        scaled(turned_hi[:, :], rot[:, 0, :]).then_inc(turned_hid, 1)
                        act.wait_ge(gate_pre, n + 1)
                        nc.scalar.activation(gate[:, :, :], gate[:, :, :], ACT.Tanh, scale=0.5).then_inc(gate_done, 1)
                        if first:
                            down_weights(0)
                            down_weights(1)
                            ffn_up_weights()
                    if s == on.norm and on.front:
                        act.wait_ge(st_1.done, n + 1)
                        norm_rows(x2n, x1, st_1, x2n_done)
                        if second:
                            ffn_down_weights()
                    if s == 7 and on.mlp:
                        act.wait_ge(st_y.done, i + 1)
                        if not isinstance(i, int) or i >= 1:
                            act.wait_ge(zb_done, i)
                        norm_rows(yn, y[par], st_y, yn_done)

            run(act, iteration)

        @block.vector
        def _(dve):
            made = [0]

            def link(ins):
                made[0] += 1
                ins.then_inc(dve_setup, 1)
                dve.wait_ge(dve_setup, made[0])

            def staged(b):
                return ps_hid[:, b, :, :].rearrange("p a n -> p (a n)")

            def stats(st, src, n):
                if not isinstance(n, int) or n >= 1:
                    dve.wait_ge(st.done, n)
                for t in range(ST):
                    last = nc.vector.bn_stats(st.raw[:, t, :], src[:, t, :])
                last.then_inc(st.bn, 1)
                dve.wait_ge(dve_setup, 1)
                dve.wait_ge(st.bn, n + 1)
                for t in range(ST):
                    last = nc.vector.bn_aggr(st.mv[:, t, :], st.raw[:, t, :])
                last.then_inc(st.agg, 1)

            link(nc.vector.memset(decay[:], 0.0))
            dve.wait_ge(x_loaded, 16)
            stats(st_x, x_in[:, 0, :, :], 0)
            dve.wait_ge(cols_ps, 1)
            nc.vector.tensor_copy(vec_cols[:], ps_aux[:, 0, 0:NROW]).then_inc(cols_done, 1)
            dve.wait_ge(cols_done, 1)
            turns, whole, coarse, fine = (tiny[:, k:k + 1] for k in range(4))
            link(nc.vector.tensor_scalar(turns, col("frequency"), INV_TWO_PI, None, ALU.mult))
            link(nc.vector.tensor_scalar(whole, turns, ROUND_TO_INT, -ROUND_TO_INT, ALU.add, ALU.add))
            link(nc.vector.tensor_tensor(turns, turns, whole, ALU.subtract))
            link(nc.vector.tensor_scalar(coarse, turns, ROUND_TO_13_BITS, -ROUND_TO_13_BITS, ALU.add, ALU.add))
            link(nc.vector.tensor_tensor(fine, turns, coarse, ALU.subtract))

            def dot(k, src, vec):
                link(nc.vector.tensor_tensor_reduce(out=junk, in0=src, in1=vec, scale=1.0, scalar=0.0,
                                                    op0=ALU.mult, op1=ALU.add, accum_out=dots[:, k:k + 1]))

            def low(dst, src, scale, hi, done=None):
                last = nc.vector.scalar_tensor_tensor(out=dst, in0=src, scalar=scale, in1=hi.bitcast(F32),
                                                      op0=ALU.mult, op1=ALU.subtract)
                if done:
                    last.then_inc(done, 1)

            dve.wait_ge(small_in, 16 * (3 + 2 * H))
            dve.wait_ge(bc_in, 16 * 4)
            dot(0, raw_in, n1_b_bc)
            for e in range(KT):
                dot(1 + e, raw_gate[:, e, :], n1_b_bc)
            a = cols["gate_b"][0]
            link(nc.vector.tensor_tensor(gate_col[:], dots[:, 1:1 + KT], vec_cols[:, a:a + KT], ALU.add))
            dve.wait_ge(const_made, 10)
            for e in range(KT):
                last = nc.vector.tensor_scalar(gate_fan[:, e, :], ident[:], 0.0, gate_col[:, e:e + 1],
                                               ALU.mult, ALU.add)
            last.then_inc(fan_done, 1)
            dve.wait_ge(prep_T, 2)
            nc.vector.tensor_scalar(outT, staged(1)[:, 0:D], 0.5, None, ALU.mult).then_inc(outT_done, 1)
            dve.wait_ge(prep_hi, 1)
            for k in range(KT):
                low(win_lo[:, k, :], staged(0)[:, k * P:(k + 1) * P], col("n1_g", k), win_hi[:, k, :])
                low(wgate_lo[:, k, :], staged(0)[:, GT + k * D:GT + (k + 1) * D], col("n1_g", k),
                    wgate_hi[:, k, :], prep_lo if k == KT - 1 else None)
            dve.wait_ge(gate_bias_ps, 1)
            nc.vector.tensor_copy(gate_bias[:], ps_aux[:, 1, 0:D]).then_inc(gate_bias_made, 1)
            pos = cos_t[:, 0:TAB]
            link(nc.vector.tensor_scalar(tab[0], pos, coarse, None, ALU.mult))
            link(nc.vector.tensor_scalar(tab[1], tab[0], ROUND_TO_INT, -ROUND_TO_INT, ALU.add, ALU.add))
            link(nc.vector.tensor_tensor(tab[0], tab[0], tab[1], ALU.subtract))
            link(nc.vector.scalar_tensor_tensor(out=tab[0], in0=pos, scalar=fine, in1=tab[0],
                                                op0=ALU.mult, op1=ALU.add))
            link(nc.vector.tensor_scalar(tab[1], tab[0], ROUND_TO_INT, -ROUND_TO_INT, ALU.add, ALU.add))
            nc.vector.tensor_tensor(tab[2], tab[0], tab[1], ALU.subtract).then_inc(tables_arg, 1)
            dve.wait_ge(tables_arg, 1)
            link(nc.vector.tensor_scalar(tab[0], tab[0], 0.25, None, ALU.add))
            link(nc.vector.tensor_scalar(tab[1], tab[0], ROUND_TO_INT, -ROUND_TO_INT, ALU.add, ALU.add))
            nc.vector.tensor_tensor(tab[0], tab[0], tab[1], ALU.subtract).then_inc(tables_arg, 1)

            def decay_table():
                dve.wait_ge(decay_tanh, 1)
                link(nc.vector.tensor_scalar(tiny[:, 6:7], tiny[:, 5:6], 0.5, 0.5, ALU.mult, ALU.add))
                link(nc.vector.tensor_scalar(decay[:], decay[:], tiny[:, 6:7], None, ALU.add))

            def out_weights():
                dve.wait_ge(prep_hi, 2)
                low(wout_lo[:, :], staged(1)[:, GT:GT + D], 1.0, wout_hi[:, :], prep_lo)

            def up_weights(k):
                dve.wait_ge(prep_hi, 3 + k)
                low(wup_lo[:, k, :], staged(k), col("n2_g", k), wup_hi[:, k, :], prep_lo)

            def up_biases():
                dve.wait_ge(w1_in, 16)
                for m in range(MT):
                    dot(1 + KT + m, raw_w1[:, m, :], n2_b_bc)
                a = cols["b1"][0]
                nc.vector.tensor_tensor(up_bias[:], dots[:, 1 + KT:], vec_cols[:, a:a + MT],
                                        ALU.add).then_inc(dots_done, 1)

            def down_weights(half):
                dve.wait_ge(prep_hi, 5 + half)
                part = slice(half * MT // 2, (half + 1) * MT // 2)
                low(wdown_lo[:, part, :].rearrange("p c d -> p (c d)"), staged(half), 1.0,
                    wdown_hi[:, part, :].rearrange("p c d -> p (c d)"), prep_lo)

            def save_starts():
                dve.wait_ge(tables_sin, 2)
                nc.vector.tensor_copy(starts[:, 0, :], cos_t[:, GT:TAB])
                nc.vector.tensor_copy(starts[:, 1, :], sin_t[:, GT:TAB]).then_inc(starts_done, 1)

            def later_tables():
                dve.wait_ge(starts_done, 1)
                c0, s0 = cos_t[:, 0:GT], sin_t[:, 0:GT]
                for q in range(1, GB):
                    part = slice(q * GT, (q + 1) * GT)
                    c, s_ = starts[:, 0, q:q + 1], starts[:, 1, q:q + 1]
                    nc.vector.tensor_scalar(rot[:, 0, :], s0, s_, None, ALU.mult)
                    link(nc.vector.tensor_scalar(rot[:, 1, :], c0, s_, None, ALU.mult))
                    nc.vector.scalar_tensor_tensor(out=cos_t[:, part], in0=c0, scalar=c, in1=rot[:, 0, :],
                                                   op0=ALU.mult, op1=ALU.subtract)
                    link(nc.vector.scalar_tensor_tensor(out=sin_t[:, part], in0=s0, scalar=c, in1=rot[:, 1, :],
                                                        op0=ALU.mult, op1=ALU.add))

            def dequantise(loaded):
                dve.wait_ge(loaded, 32)
                nc.vector.scalar_tensor_tensor(out=q_raw, in0=q_raw.bitcast(I32), scalar=-128.0, in1=q_scale,
                                               op0=ALU.add, op1=ALU.mult).then_inc(deq_done, 1)

            def ffn_up_weights():
                dve.wait_ge(fhi_done, 1)
                for k in range(KT):
                    low(fup_lo[:, k, :], q_raw[:, k * M:(k + 1) * M], col("gamma", k), fup_hi[:, k, :],
                        flo_done if k == KT - 1 else None)

            def ffn_up_bias():
                dve.wait_ge(fbias_ps, 1)
                b = cols["fb1"][0]
                nc.vector.tensor_tensor(fup_bias[:], ps_aux[:, 0, 0:MT], vec_cols[:, b:b + MT],
                                        ALU.add).then_inc(setup_bias, 1)

            def ffn_down_weights():
                dequantise(q2_in)
                link(nc.vector.tensor_scalar(fc2_half[:], fc2_b_bc, 0.5, None, ALU.mult))
                dve.wait_ge(fhi_done, 2)
                low(fdown_lo[:, :, :].rearrange("p c d -> p (c d)"), q_raw, 0.5,
                    fdown_hi[:, :, :].rearrange("p c d -> p (c d)"), flo_done)

            def wide(buf):
                return buf.rearrange("p a n -> p (a n)")

            def low_of_aux(dst, hi, done):
                nc.vector.tensor_tensor(wide(dst[:, :, :]), wide(ps_aux[:, :, :]),
                                        wide(hi[:, :, :]).bitcast(F32), ALU.subtract).then_inc(done, 1)

            def low_of_hidden(i, s):
                k = step(i, s)
                dve.wait_ge(act_done, k + 1)
                if not isinstance(k, int) or k >= 2:
                    dve.wait_ge(down_done, k - 1)
                nc.vector.tensor_tensor(wide(hid_lo[:, s % 2, :, :]), wide(hid),
                                        wide(hid_hi[:, s % 2, :, :]).bitcast(F32),
                                        ALU.subtract).then_inc(lo_done, 1)

            def iteration(i, par, on):
                n = i + 1
                first = isinstance(i, int) and i == -1
                second = isinstance(i, int) and i == 0
                for s in range(SLOTS):
                    if s == on.turn2 and on.front:
                        dve.wait_ge(x1T_hid, n + 1)
                        low_of_aux(x1T_lo, x1T_hi, x1T_lod)
                    if s in on.slots():
                        low_of_hidden(i, s)
                    if s == 0 and on.ffn:
                        dve.wait_ge(yT_hid, i)
                        low_of_aux(yT_lo, yT_hi, yT_lod)
                    if s == 0 and on.final:
                        dve.wait_ge(down_done, step(i - 1, SLOTS - 1) + 1)
                        nc.vector.tensor_tensor(zb, ps_acc[:, :, :], zb, ALU.add).then_inc(z_done, 1)
                        dve.wait_ge(z_done, i - 1)
                        if not isinstance(i, int) or i > 2:
                            dve.wait_ge(z_scaled, i - 2)
                        stats(st_z, zb, i - 2)
                    if s == on.turn and on.front:
                        if first:
                            out_weights()
                        dve.wait_ge(xT_hid, n + 1)
                        low_of_aux(xT_lo, xT_hi, xT_lod)
                        if first:
                            up_weights(0)
                            decay_table()
                            save_starts()
                    if s == on.beta and on.front:
                        if isinstance(n, int):
                            table = slice(n % GB * GT, (n % GB + 1) * GT)
                            place = slice(n % GB, n % GB + 1)
                        else:
                            table = bass.ts(n % GB, GT)
                            place = bass.ts(n % GB, 1)
                        halves = ((slice(0, K), slice(K, K2)), (slice(K, K2), slice(0, K)))
                        dve.wait_ge(beta_ps, n + 1)
                        nc.vector.scalar_tensor_tensor(out=rot[:, 0, :], in0=ps_aux[:, 0, :], scalar=beta_bias,
                                                       in1=cos_t[:, table], op0=ALU.add, op1=ALU.mult)
                        for to, of in halves:
                            last = nc.vector.scalar_tensor_tensor(
                                out=rot[to, 1, :], in0=ps_aux[of, 0, :], scalar=beta_bias[of, :],
                                in1=sin_t[of, table], op0=ALU.add, op1=ALU.mult)
                        last.then_inc(rot_done, 1)
                        dve.wait_ge(rot_done, n + 1)
                        nc.vector.tensor_tensor(rot[:, 0, :], rot[:, 0, :], rot[:, 1, :],
                                                ALU.add).then_inc(turned_in, 1)
                        if isinstance(n, int) and n == 0:
                            start = 0.0
                        else:
                            nc.vector.tensor_tensor(carry[:], scanned[:, GT - 1:GT], carry_mask[:, place],
                                                    ALU.mult).then_inc(carry_done, 1)
                            dve.wait_ge(carry_done, n)
                            start = carry[:]
                        dve.wait_ge(turned_in, n + 1)
                        nc.vector.tensor_tensor_scan(scanned[:], decay[:], rot[:, 0, :], start, ALU.mult,
                                                     ALU.add).then_inc(scan_done, 1)
                        dve.wait_ge(scan_done, n + 1)
                        nc.vector.tensor_tensor(rot[:, 0, :], scanned[:], cos_t[:, table], ALU.mult)
                        for to, of in halves:
                            last = nc.vector.tensor_tensor(rot[to, 1, :], scanned[of, :], sin_t[of, table], ALU.mult)
                        last.then_inc(back_parts, 1)
                        dve.wait_ge(back_parts, n + 1)
                        nc.vector.tensor_tensor(rot[:, 0, :], rot[:, 0, :], rot[:, 1, :],
                                                ALU.subtract).then_inc(back_done, 1)
                    if s == on.gate and on.front:
                        if first:
                            up_weights(1)
                        dve.wait_ge(turned_hid, n + 1)
                        nc.vector.tensor_tensor(turned_lo[:, :], rot[:, 0, :], turned_hi[:, :].bitcast(F32),
                                                ALU.subtract).then_inc(turned_lod, 1)
                        dve.wait_ge(gate_ps, n + 1)
                        nc.vector.tensor_tensor(gate[:, :, :], aux_rows, over_rows(gate_bias[:]),
                                                ALU.add).then_inc(gate_pre, 1)
                        if first:
                            up_biases()
                            down_weights(0)
                    if s == on.out and on.front:
                        dve.wait_ge(gate_done, n + 1)
                        dve.wait_ge(out_ps, n + 1)
                        nc.vector.scalar_tensor_tensor(out=gate[:, :, :], in0=gate[:, :, :], scalar=1.0,
                                                       in1=aux_rows, op0=ALU.add, op1=ALU.mult).then_inc(gated, 1)
                    if s == 4 and on.mlp:
                        dve.wait_ge(down_done, step(i, PAIRS - 1) + 1)
                        dve.wait_ge(x1b_done, i + 1)
                        nc.vector.tensor_tensor(x1b, ps_acc[:, :, :], x1b, ALU.add).then_inc(x2_done, 1)
                    if s == on.out and on.front:
                        dve.wait_ge(gated, n + 1)
                        if on.mlp:
                            dve.wait_ge(x1b_done, n)
                            dve.wait_ge(x2n_done, n)
                        for t in range(ST):
                            last = nc.vector.scalar_tensor_tensor(
                                out=x1[:, t, :], in0=xn[:, t, :], scalar=st_x.ratio[:, t:t + 1],
                                in1=gate[:, t, :], op0=ALU.mult, op1=ALU.add)
                        last.then_inc(x1_done, 1)
                        dve.wait_ge(x1_done, n + 1)
                        stats(st_1, x1, n)
                        if first:
                            down_weights(1)
                            dequantise(q1_in)
                            later_tables()
                            ffn_up_weights()
                    if s == 4 and on.mlp:
                        dve.wait_ge(x2_done, i + 1)
                        stats(st_2, x1b, i)
                        if second:
                            ffn_down_weights()
                    if s == 5 and on.ffn:
                        if on.final:
                            dve.wait_ge(stored, 16 * (i - 1))
                        for t in range(ST):
                            last = nc.vector.scalar_tensor_tensor(
                                out=zb[:, t, :], in0=yn[:, t, :], scalar=st_y.ratio[:, t:t + 1],
                                in1=fc2_half[:], op0=ALU.mult, op1=ALU.add)
                        last.then_inc(zb_done, 1)
                    if s == 5 and on.mlp:
                        dve.wait_ge(st_2.done, i + 1)
                        if on.final:
                            dve.wait_ge(out_done, i - 1)
                        if second:
                            dve.wait_ge(flo_done, 2)
                        for t in range(ST):
                            last = nc.vector.scalar_tensor_tensor(
                                out=y[par][:, t, :], in0=x1b[:, t, :], scalar=st_2.r[:, t:t + 1],
                                in1=x_in[:, par, t, :], op0=ALU.mult, op1=ALU.add)
                        last.then_inc(y_done, 1)
                    if s == 6 and on.mlp:
                        dve.wait_ge(y_done, i + 1)
                        stats(st_y, y[par], i)
                    if s == 7 and first:
                        ffn_up_bias()
                    if s == 7 and on.next_stat:
                        dve.wait_ge(x_loaded, 16 * (i + 3))
                        stats(st_x, x_in[:, par, :, :], i + 2)

            run(dve, iteration)


_INS = ["L0_attn_x", "L0_attn_in_proj_w", "L0_attn_log_decay", "L0_attn_frequency", "L0_attn_coupling",
        "L0_attn_out_proj_w", "L0_attn_gate_w", "L0_attn_gate_b", "L0_attn_n1_g", "L0_attn_n1_b",
        "L0_attn_n2_g", "L0_attn_n2_b", "L0_attn_mlp_w1", "L0_attn_mlp_b1", "L0_attn_mlp_w2", "L0_attn_mlp_b2",
        "L0_ffn_ln_gamma", "L0_ffn_ln_beta", "L0_ffn_fc1_q", "L0_ffn_fc1_scales", "L0_ffn_fc1_bias",
        "L0_ffn_fc2_q", "L0_ffn_fc2_scales", "L0_ffn_fc2_bias"]


def kernel(**inputs):
    import numpy as np
    import concourse.bacc as bacc
    from concourse.bass_utils import run_bass_kernel_spmd

    nc = bacc.Bacc("TRN2", target_bir_lowering=False, num_devices=1)
    arrays, args = {}, []
    for name in _INS:
        a = np.ascontiguousarray(inputs[name])
        arrays[f"in_{name}"] = a
        args.append(nc.dram_tensor(f"in_{name}", a.shape, mybir.dt.from_np(a.dtype), kind="ExternalInput").ap())
    shape = arrays["in_L0_attn_x"].shape
    out = nc.dram_tensor("out", shape, F32, kind="ExternalOutput").ap()
    build(nc, *args, out)
    r = run_bass_kernel_spmd(nc, [arrays], core_ids=[0])
    return r.results[0]["out"]
```

```python
from contextlib import ExitStack

import concourse.bass as bass
from concourse import mybir

F32 = mybir.dt.float32
F32R = mybir.dt.float32r
I32 = mybir.dt.int32
ALU = mybir.AluOpType
ACT = mybir.ActivationFunctionType

P = 128
EPS = 1e-5
ROUND_TO_INT = 12582912.0
ROUND_TO_13_BITS = 1536.0
INV_TWO_PI = 0.15915494309189535
TURN = 6.283185


def build(nc, x, in_proj_w, log_decay, frequency, coupling, out_proj_w, gate_w, gate_b, n1_g, n1_b,
          n2_g, n2_b, mlp_w1, mlp_b1, mlp_w2, mlp_b2, ln_gamma, ln_beta, fc1_q, fc1_scales, fc1_bias,
          fc2_q, fc2_scales, fc2_bias, out):
    B, T, D = x.shape
    K2 = in_proj_w.shape[0]
    K = K2 // 2
    H, KH, _ = coupling.shape
    M = mlp_w1.shape[0]
    KT = D // P
    MT = M // P
    PAIRS = MT // 2
    GT = 512
    ST = GT // P
    G = B * T // GT
    GB = T // GT
    SLOTS = 2 * PAIRS
    assert K2 == P and GT == 512 and D == 256 and fc1_q.shape == (D, M) and fc1_scales.shape[0] == KT
    assert GB == 4 and G == 16

    x_rows = x.rearrange("b (g t p) d -> (b g) p t d", t=ST, p=P)
    out_rows = out.rearrange("b (g t p) d -> (b g) p t d", t=ST, p=P)

    with ExitStack() as ctx:
        def sb(name, shape, dt=F32):
            return ctx.enter_context(nc.sbuf_tensor(name, shape, dt))

        def sem(name):
            return ctx.enter_context(nc.semaphore(name))

        win_hi, win_lo = (sb(f"win_{h}", [P, KT, P], F32R) for h in ("hi", "lo"))
        wgate_hi, wgate_lo = (sb(f"wgate_{h}", [P, KT, D], F32R) for h in ("hi", "lo"))
        wout_hi, wout_lo = (sb(f"wout_{h}", [P, D], F32R) for h in ("hi", "lo"))
        wup_hi, wup_lo = (sb(f"wup_{h}", [P, KT, M], F32R) for h in ("hi", "lo"))
        wdown_hi, wdown_lo = (sb(f"wdown_{h}", [P, MT, D], F32R) for h in ("hi", "lo"))
        fup_hi, fup_lo = (sb(f"fup_{h}", [P, KT, M], F32R) for h in ("hi", "lo"))
        fdown_hi, fdown_lo = (sb(f"fdown_{h}", [P, MT, D], F32R) for h in ("hi", "lo"))

        ident = sb("ident", [P, P])
        cos_t = sb("cos_t", [P, T])
        sin_t = sb("sin_t", [P, T])
        decay = sb("decay", [P, GT])
        gate_bias = sb("gate_bias", [P, D])
        vec_bc = sb("vec_bc", [P, 4, D])
        n1_b_bc, n2_b_bc, mlp_b2_bc, fc2_b_bc = (vec_bc[:, k, :] for k in range(4))
        coup = sb("coup", [P, P])
        coup_raw = sb("coup_raw", [P, KH])
        carry_mask = sb("carry_mask", [P, GB])
        half_power = sb("half_power", [P, 2, ST])
        early = (("n1_g", n1_g, KT), ("gate_b", gate_b, KT), ("log_decay", log_decay, 1), ("frequency", frequency, 1))
        rest = (("n2_g", n2_g, KT), ("gamma", ln_gamma, KT), ("beta", ln_beta, KT), ("b1", mlp_b1, MT),
                ("fb1", fc1_bias, MT))
        NEARLY, NREST = (sum(n for _, _, n in batch) for batch in (early, rest))
        NROW = NEARLY + NREST
        early_rows, rest_rows = sb("early_rows", [NEARLY, P]), sb("rest_rows", [NREST, P])
        vec_cols = sb("vec_cols", [P, NROW])
        r0 = 0
        cols = {}
        for name, _, n in early + rest:
            cols[name] = (r0, n)
            r0 += n

        def col(name, k=0):
            return vec_cols[:, cols[name][0] + k:cols[name][0] + k + 1]

        eps_tile = sb("eps_tile", [P, ST])
        dots = sb("dots", [P, 1 + KT + MT])
        beta_bias = dots[:, 0:1]
        gate_col = sb("gate_col", [P, KT])
        up_bias = sb("up_bias", [P, MT])
        fup_bias = sb("fup_bias", [P, MT])
        zero_point = sb("zero_point", [P, 1])
        tiny = sb("tiny", [P, 8])
        fc2_half = sb("fc2_half", [P, D])

        x_in = sb("x_in", [P, 2, ST, D])
        xn = sb("xn", [P, ST, D])
        xT_hi, xT_lo = (sb(f"xT_{h}", [P, KT, GT], F32R) for h in ("hi", "lo"))
        rot = sb("rot", [P, 2, GT])
        scanned = sb("scanned", [P, GT])
        turned_hi, turned_lo = (sb(f"turned_{h}", [P, GT], F32R) for h in ("hi", "lo"))
        gate = sb("gate", [P, ST, D])
        mid = sb("mid", [P, 4, ST * D])
        x1, x1b, x2n = (mid[:, k, :].rearrange("p (t d) -> p t d", d=D) for k in range(3))
        hid = mid[:, 3, :].rearrange("p (m n) -> p m n", n=GT)
        x1T_hi, x1T_lo = (sb(f"x1T_{h}", [P, KT, GT], F32R) for h in ("hi", "lo"))
        hid_hi, hid_lo = (sb(f"hid_{h}", [P, 2, 2, GT], F32R) for h in ("hi", "lo"))
        late = sb("late", [P, 4, ST * D])
        y = [late[:, k, :].rearrange("p (t d) -> p t d", d=D) for k in (0, 2)]
        yn, zb = (late[:, k, :].rearrange("p (t d) -> p t d", d=D) for k in (1, 3))
        yT_hi, yT_lo = (sb(f"yT_{h}", [P, KT, GT], F32R) for h in ("hi", "lo"))
        carry = sb("carry", [P, 1])

        y_shift = [sb(f"y_shift{k}", [P, ST]) for k in range(2)]

        class Stat:
            def __init__(self, name, double, ahead=0):
                self.ahead = ahead
                self.raw = sb(f"{name}_raw", [P, ST, 6])
                self.mv = sb(f"{name}_mv", [P, ST, 2])
                self.var = sb(f"{name}_var", [P, 2, ST])
                self.r = sb(f"{name}_r", [P, ST])
                self.parts = sb(f"{name}_parts", [P, 2, ST])
                self.neg = sb(f"{name}_neg", [P, ST])
                self.shift = sb(f"{name}_shift", [P, ST])
                self.ratio = sb(f"{name}_ratio", [P, ST])
                self.double = double
                self.bn = sem(f"{name}_bn")
                self.agg = sem(f"{name}_agg")
                self.eps = sem(f"{name}_eps")
                self.powd = sem(f"{name}_powd")
                self.done = sem(f"{name}_done")
                self.partsd = sem(f"{name}_partsd")
                self.ratiod = sem(f"{name}_ratiod")

        st_x, st_1, st_2, st_y = (Stat(n, d) for n, d in (("sx", True), ("s1", False), ("s2", False), ("sy", True)))
        st_z = Stat("sz", False, ahead=1)

        raw_w1 = [tab[:, 2 * GT:4 * GT].rearrange("p (c d) -> p c d", d=D) for tab in (cos_t, sin_t)]

        def w1_rows(c):
            return raw_w1[c // ST][:, c % ST, :]

        raw_w2 = [mid[:, 2 + half, :].rearrange("p (e m) -> p e m", e=KT) for half in range(2)]
        flat = late[:, :, :].rearrange("p a b -> p (a b)")
        raw_in = flat[:, 0:D]
        raw_gate = flat[:, 2 * D:2 * D + KT * D].rearrange("p (e d) -> p e d", d=D)
        raw_out = flat[:, 4 * D:5 * D].rearrange("p (e k) -> p e k", k=P)
        outT = flat[:, 5 * D:6 * D]
        junk = rot[:, 1, 0:D]
        gate_fan = flat[:, 7 * D:8 * D].rearrange("p (e q) -> p e q", q=P)
        TAB = GT + GB
        tab = [flat[:, 8 * D + k * TAB:8 * D + (k + 1) * TAB] for k in range(3)]
        starts = sb("starts", [P, 2, GB])
        ffn_up = sb("ffn_up", [P, KT * M])
        ffn_scale = late[:, 0:2, :].rearrange("p a b -> p (a b)")
        ffn_down = late[:, 2:4, :].rearrange("p a b -> p (a b)")

        ps_hid = ctx.enter_context(nc.psum_tensor("ps_hid", [P, 2, 2, GT], F32))
        ps_acc = ctx.enter_context(nc.psum_tensor("ps_acc", [P, ST, D], F32))
        ps_aux = ctx.enter_context(nc.psum_tensor("ps_aux", [P, 2, GT], F32))
        aux_rows = ps_aux[:, :, :].rearrange("p a (s d) -> p (a s) d", d=D)

        rows_in = sem("rows_in")
        bc_in = sem("bc_in")
        rest_in = sem("rest_in")
        rest_bc_in = sem("rest_bc_in")
        small_in = sem("small_in")
        coup_lower = sem("coup_lower")
        coup_made = sem("coup_made")
        w1_in, w2_in = sem("w1_in"), sem("w2_in")
        q1_in, q2_in = sem("q1_in"), sem("q2_in")
        scales1_in, scales2_in = sem("scales1_in"), sem("scales2_in")
        x_loaded = sem("x_loaded")
        stored = sem("stored")
        const_made = sem("const_made")
        ident_zero = sem("ident_zero")
        dve_setup = sem("dve_setup")
        cols_ps, cols_done = sem("cols_ps"), sem("cols_done")
        prep_T = sem("prep_T")
        prep_hi = sem("prep_hi")
        prep_lo = sem("prep_lo")
        outT_done = sem("outT_done")
        gate_col_made = sem("gate_col_made")
        fan_done = sem("fan_done")
        decay_made = sem("decay_made")
        decay_along = sem("decay_along")
        gate_bias_made = sem("gate_bias_made")
        gate_bias_ps = sem("gate_bias_ps")
        tables_arg = sem("tables_arg")
        tables_sin = sem("tables_sin")
        starts_done = sem("starts_done")
        decay_tanh = sem("decay_tanh")
        centred = sem("centred")
        deq_done = sem("deq_done")
        fhi_done = sem("fhi_done")
        flo_done = sem("flo_done")
        fbias_ps = sem("fbias_ps")
        up_bias_made = sem("up_bias_made")
        fup_bias_made = sem("fup_bias_made")

        xn_done = sem("xn_done")
        xT_ps = sem("xT_ps")
        xT_hid, xT_lod = sem("xT_hid"), sem("xT_lod")
        beta_ps = sem("beta_ps")
        rot_done = sem("rot_done")
        turned_in = sem("turned_in")
        back_parts = sem("back_parts")
        scan_done = sem("scan_done")
        carry_done = sem("carry_done")
        back_done = sem("back_done")
        turned_hid, turned_lod = sem("turned_hid"), sem("turned_lod")
        gate_ps = sem("gate_ps")
        gate_pre = sem("gate_pre")
        gate_done = sem("gate_done")
        out_ps = sem("out_ps")
        gated = sem("gated")
        x1_done = sem("x1_done")
        x1b_done = sem("x1b_done")
        x2n_done = sem("x2n_done")
        x1T_ps = sem("x1T_ps")
        x1T_hid, x1T_lod = sem("x1T_hid"), sem("x1T_lod")
        up_done = sem("up_done")
        act_done = sem("act_done")
        lo_done = sem("lo_done")
        down_done = sem("down_done")
        x2_done = sem("x2_done")
        y_done = sem("y_done")
        yn_done = sem("yn_done")
        yT_ps = sem("yT_ps")
        yT_hid, yT_lod = sem("yT_hid"), sem("yT_lod")
        zb_done = sem("zb_done")
        z_done = sem("z_done")
        z_shift = sem("z_shift")
        y_shift_done = sem("y_shift_done")
        z_scaled = sem("z_scaled")
        last_bank = sem("last_bank")
        last_sum = sem("last_sum")
        out_done = sem("out_done")

        def step(i, s):
            if isinstance(i, int) and (i == 0 or i == G):
                return s if i == 0 else SLOTS * G - 2 * PAIRS + s
            return i * SLOTS + (s - PAIRS)

        def over_rows(vec):
            return vec.unsqueeze(1).to_broadcast([P, ST, D])

        class Stages:
            def __init__(self, front=True, mlp=True, ffn=True, final=True, next_stat=True,
                         turn_y=0, turn=1, beta=2, gate=3, out=4, norm=6, turn2=7, close=2):
                self.front, self.mlp, self.ffn, self.final, self.next_stat = front, mlp, ffn, final, next_stat
                self.turn_y = turn_y
                self.turn, self.beta, self.gate, self.out = turn, beta, gate, out
                self.norm, self.turn2, self.close = norm, turn2, close

            def slots(self):
                return [s for s in range(SLOTS) if (self.mlp if s < PAIRS else self.ffn)]

        def stages(i):
            on = dict(front=i + 1 < G, mlp=0 <= i < G, ffn=1 <= i <= G, final=2 <= i, next_stat=i + 2 < G)
            if i == 0:
                on.update(turn=-0.5, beta=0, gate=1, out=2, norm=3, turn2=4)
            if i == 1:
                on.update(turn_y=2.5, turn=3, beta=3.5, gate=4, out=5)
            if i == G:
                on.update(close=PAIRS)
            return Stages(**on)

        LOOP_FROM, LOOP_TO = 2, G - 2

        def run(eng, iteration):
            for i in range(-1, LOOP_FROM):
                iteration(i, i % 2, stages(i))
            with eng.Fori(0, (LOOP_TO - LOOP_FROM) // 2) as j:
                for u in range(2):
                    iteration(j * 2 + (LOOP_FROM + u), u, Stages())
            for i in range(LOOP_TO, G + 2):
                iteration(i, i % 2, stages(i))

        block = ctx.enter_context(nc.Block())

        @block.sync
        def _(sp):
            def load_x(n, par):
                sp.dma_start(x_in[:, par, :, :], x_rows[n]).then_inc(x_loaded, 16)

            def rows(dst, batch, loaded):
                a = 0
                for _, vec, n in batch:
                    if vec.shape[0] == n * P:
                        sp.dma_start(dst[a:a + n, :], vec.rearrange("(k p) -> k p", p=P)).then_inc(loaded, 16)
                    else:
                        for half in range(2):
                            sp.dma_start(dst[a:a + 1, half * K:(half + 1) * K],
                                         vec.rearrange("(a k) -> a k", a=1)).then_inc(loaded, 16)
                    a += n

            load_x(0, 0)
            rows(early_rows, early, rows_in)
            sp.dma_start(vec_bc[:, 0, :], n1_b.partition_broadcast(P)).then_inc(bc_in, 16)
            w1_parts = mlp_w1.rearrange("(a c p) d -> a p c d", a=2, p=P)
            for half in range(2):
                sp.dma_start(raw_w1[half], w1_parts[half]).then_inc(w1_in, 16)
            rows(rest_rows, rest, rest_in)
            for k, vec in enumerate((n2_b, mlp_b2, fc2_bias)):
                sp.dma_start(vec_bc[:, 1 + k, :], vec.partition_broadcast(P)).then_inc(rest_bc_in, 16)
            w2_parts = mlp_w2.rearrange("(e p) (h m) -> h p e m", p=P, h=2)
            for half in range(2):
                sp.dma_start(raw_w2[half], w2_parts[half]).then_inc(w2_in, 16)
            sp.wait_ge(st_x.agg, 1)
            load_x(1, 1)
            sp.dma_start(ffn_up[:, :].bitcast(I32).rearrange("p (k m) -> p k m", m=M),
                         fc1_q.rearrange("(k p) m -> p k m", p=P)).then_inc(q1_in, 16)
            sp.wait_ge(prep_T, 3)
            sp.wait_ge(gate_bias_ps, 1)
            sp.dma_start(ffn_scale.rearrange("p (k m) -> p k m", m=M),
                         fc1_scales.partition_broadcast(P)).then_inc(scales1_in, 16)
            sp.wait_ge(tables_sin, 2)
            sp.dma_start(ffn_down.bitcast(I32).rearrange("p (c d) -> p c d", d=D),
                         fc2_q.rearrange("(c p) d -> p c d", p=P)).then_inc(q2_in, 16)
            sp.wait_ge(deq_done, 1)
            sp.dma_start(ffn_scale.rearrange("p (c d) -> p c d", d=D),
                         fc2_scales.partition_broadcast(P)).then_inc(scales2_in, 16)

            def iteration(i, par, on):
                if isinstance(i, int) and i == G + 1:
                    for t in range(ST):
                        sp.wait_ge(out_done, G + t)
                        sp.dma_start(out_rows[i - 2, :, t, :], zb[:, t, :]).then_inc(stored, 16)
                elif on.final:
                    sp.wait_ge(out_done, i - 1)
                    sp.dma_start(out_rows[i - 2], zb).then_inc(stored, 16)
                if on.mlp and on.next_stat:
                    sp.wait_ge(y_done, i + 1)
                    sp.dma_start(x_in[:, par, :, :], x_rows[i + 2]).then_inc(x_loaded, 16)

            run(sp, iteration)
            sp.wait_ge(stored, 16 * (G - 1 + ST))

        @block.gpsimd
        def _(pool):
            nc.gpsimd.memset(st_z.shift[:, :], 0.0).then_inc(st_z.done, 1)
            nc.gpsimd.memset(ident[:], 0.0).then_inc(ident_zero, 1)
            pool.wait_ge(ident_zero, 1)
            nc.gpsimd.affine_select(out=ident[:], in_=ident[:], compare_op=ALU.not_equal, fill=1.0, base=0,
                                    pattern=[[-1, P]], channel_multiplier=1).then_inc(const_made, 1)
            nc.gpsimd.memset(eps_tile[:], EPS).then_inc(const_made, 1)
            nc.gpsimd.memset(half_power[:, 0, :], -0.5).then_inc(const_made, 1)
            nc.gpsimd.memset(half_power[:, 1, :], 0.5).then_inc(const_made, 1)
            nc.gpsimd.memset(carry_mask[:, 0:1], 0.0).then_inc(const_made, 1)
            nc.gpsimd.memset(carry_mask[:, 1:GB], 1.0).then_inc(const_made, 1)
            nc.gpsimd.memset(tiny[:, 4:5], -TURN).then_inc(const_made, 1)
            nc.gpsimd.memset(zero_point[:, :], -128.0).then_inc(const_made, 1)
            nc.gpsimd.iota(cos_t[:, 0:GT], pattern=[[1, GT]], base=0, channel_multiplier=0,
                           allow_small_or_imprecise_dtypes=True).then_inc(const_made, 1)
            nc.gpsimd.iota(cos_t[:, GT:TAB], pattern=[[GT, GB]], base=0, channel_multiplier=0,
                           allow_small_or_imprecise_dtypes=True).then_inc(const_made, 1)
            pool.wait_ge(const_made, 10)
            nc.gpsimd.memset(tiny[K:K2, 4:5], TURN).then_inc(const_made, 1)
            pool.wait_ge(const_made, 11)

            def stat(st, n, free):
                pool.wait_ge(st.agg, n + 1)
                free()
                last = nc.gpsimd.tensor_tensor(st.var[:, 0, :], st.mv[:, :, 1], eps_tile[:, :], ALU.add)
                if st.double:
                    last = nc.gpsimd.tensor_scalar(st.var[:, 1, :], st.mv[:, :, 1], 1.0 + EPS, EPS * EPS,
                                                   ALU.mult, ALU.add)
                last.then_inc(st.eps, 1)
                nc.gpsimd.tensor_scalar(st.neg[:, :], st.mv[:, :, 0], -1.0, 0.0, ALU.mult, ALU.add)
                pool.wait_ge(st.eps, n + 1)
                nc.gpsimd.tensor_tensor(st.r[:, :], st.var[:, 1 if st.double else 0, :], half_power[:, 0, :],
                                        ALU.pow).then_inc(st.powd, 1)
                pool.wait_ge(st.powd, n + 1)
                nc.gpsimd.tensor_tensor(st.shift[:, :], st.neg[:, :], st.r[:, :], ALU.mult).then_inc(st.done, 1)
                if st.double:
                    nc.gpsimd.tensor_tensor(st.parts[:, :, :], st.var[:, :, :], half_power[:, :, :],
                                            ALU.pow).then_inc(st.partsd, 1)
                    pool.wait_ge(st.partsd, n + 1)
                    nc.gpsimd.tensor_tensor(st.ratio[:, :], st.parts[:, 0, :], st.parts[:, 1, :],
                                            ALU.mult).then_inc(st.ratiod, 1)

            def free_x(n):
                def f():
                    if not isinstance(n, int) or n > 0:
                        pool.wait_ge(xn_done, n)
                        pool.wait_ge(x1_done, n)
                return f

            def couple():
                blocks = coup[:, :].rearrange("p (h k) -> p h k", k=KH)
                pool.wait_ge(small_in, 16 * 5)
                nc.gpsimd.affine_select(out=blocks, in_=coup_raw[:, :].unsqueeze(1).to_broadcast([P, 2 * H, KH]),
                                        compare_op=ALU.is_ge, fill=0.0, base=0, pattern=[[-KH, 2 * H], [0, KH]],
                                        channel_multiplier=1).then_inc(coup_lower, 1)
                pool.wait_ge(coup_lower, 1)
                nc.gpsimd.affine_select(out=blocks, in_=blocks, compare_op=ALU.is_ge, fill=0.0, base=KH - 1,
                                        pattern=[[KH, 2 * H], [0, KH]],
                                        channel_multiplier=-1).then_inc(coup_made, 1)

            def dequantise(k, w, scales_in):
                pool.wait_ge(centred, k + 1)
                pool.wait_ge(scales_in, 16)
                nc.gpsimd.tensor_tensor(w, w, ffn_scale, ALU.mult).then_inc(deq_done, 1)

            stat(st_x, 0, free_x(0))
            couple()
            dequantise(0, ffn_up[:, :], scales1_in)

            def iteration(i, par, on):
                if on.final:
                    def free_z():
                        pool.wait_ge(z_scaled, i - 1)
                    stat(st_z, i - 2, free_z)
                    pool.wait_ge(y_shift_done, i - 1)
                    pool.wait_ge(st_z.done, i)
                    nc.gpsimd.tensor_tensor(st_z.neg[:, :], st_z.shift[:, :], y_shift[par][:, :],
                                            ALU.add).then_inc(z_shift, 1)
                    if not isinstance(i, int) or i != G + 1:
                        pool.wait_ge(z_scaled, i)
                        nc.gpsimd.tensor_tensor(zb, zb, y[par], ALU.add).then_inc(out_done, 1)
                if on.front:
                    def free_1():
                        if not isinstance(i, int) or i >= 0:
                            pool.wait_ge(x2n_done, i + 1)
                    stat(st_1, i + 1, free_1)
                if on.mlp:
                    def free_2():
                        if not isinstance(i, int) or i > 0:
                            pool.wait_ge(y_done, i)
                    stat(st_2, i, free_2)
                    nc.gpsimd.tensor_tensor(y_shift[par][:, :], st_2.neg[:, :], st_2.r[:, :], ALU.mult).then_inc(
                        y_shift_done, 1)

                    def free_y():
                        if not isinstance(i, int) or i > 0:
                            pool.wait_ge(yn_done, i)
                            pool.wait_ge(zb_done, i)
                    stat(st_y, i, free_y)
                if isinstance(i, int) and i == -1:
                    stat(st_x, 1, free_x(1))
                if on.front:
                    pool.wait_ge(x1_done, i + 2)
                    if on.mlp:
                        pool.wait_ge(y_done, i + 1)
                    if isinstance(i, int) and i == -1:
                        pool.wait_ge(rest_bc_in, 16 * 3)
                    nc.gpsimd.tensor_tensor(x1b, x1, over_rows(mlp_b2_bc), ALU.add).then_inc(x1b_done, 1)
                if on.next_stat and not (isinstance(i, int) and i == -1):
                    stat(st_x, i + 2, free_x(i + 2))
                if isinstance(i, int) and i == -1:
                    dequantise(1, ffn_down, scales2_in)

            run(pool, iteration)

        @block.tensor
        def _(pe):
            def transpose(dst, src):
                k = src.partition_size()
                return nc.tensor.transpose(dst, src, ident[0:k, 0:k])

            def staged(b):
                return ps_hid[:, b, :, :].rearrange("p a n -> p (a n)")

            pe.wait_ge(const_made, 11)
            pe.wait_ge(rows_in, 16 * 6)
            transpose(ps_acc[:, 0, 0:NEARLY], early_rows[:, :]).then_inc(cols_ps, 1)
            pe.wait_ge(small_in, 16 * 5)
            for k in range(KT):
                transpose(staged(0)[:, k * P:(k + 1) * P], raw_in[:, k * P:(k + 1) * P])
            for k in range(KT):
                for e in range(KT):
                    last = transpose(staged(0)[:, GT + (2 * k + e) * P:GT + (2 * k + e + 1) * P],
                                     raw_gate[:, e, k * P:(k + 1) * P])
            last.then_inc(prep_T, 1)
            for e in range(KT):
                last = transpose(staged(1)[:, e * P:(e + 1) * P], raw_out[:, e, :])
            last.then_inc(prep_T, 1)

            def couple_output():
                pe.wait_ge(coup_made, 1)
                pe.wait_ge(outT_done, 1)
                nc.tensor.matmul(staged(1)[:, GT:GT + D], coup[:], outT, start=True, stop=True).then_inc(prep_T, 1)

            def spread_gate_bias():
                pe.wait_ge(fan_done, 1)
                for e in range(KT):
                    last = nc.tensor.matmul(ps_acc[:, 1, e * P:(e + 1) * P], gate_fan[:, e, :], ident[:],
                                            start=True, stop=True)
                last.then_inc(gate_bias_ps, 1)

            def turn_rest_rows():
                pe.wait_ge(rest_in, 16 * 5)
                transpose(ps_acc[:, 2, 0:NREST], rest_rows[:, :]).then_inc(cols_ps, 1)

            def turn_up_weights(k):
                pe.wait_ge(w1_in, 32)
                pe.wait_ge(prep_hi, 1 + k)
                pe.wait_ge(prep_lo, 1 + k)
                for c in range(MT):
                    last = transpose(staged(k)[:, c * P:(c + 1) * P], w1_rows(c)[:, k * P:(k + 1) * P])
                last.then_inc(prep_T, 1)

            def turn_down_weights(half):
                pe.wait_ge(w2_in, 32)
                pe.wait_ge(prep_hi, 3 + half)
                pe.wait_ge(prep_lo, 3 + half)
                for c in range(MT // 2):
                    for e in range(KT):
                        last = transpose(staged(half)[:, (KT * c + e) * P:(KT * c + e + 1) * P],
                                         raw_w2[half][:, e, c * P:(c + 1) * P])
                last.then_inc(prep_T, 1)

            def ffn_bias():
                pe.wait_ge(deq_done, 1)
                pe.wait_ge(cols_done, 2)
                pe.wait_ge(gate_bias_made, 1)
                for m in range(MT):
                    for k in range(KT):
                        last = nc.tensor.matmul(ps_acc[:, 0, m:m + 1], ffn_up[:, k * M + m * P:k * M + (m + 1) * P],
                                                col("beta", k), start=(k == 0), stop=(k == KT - 1))
                last.then_inc(fbias_ps, 1)

            def turn_rows(src, done):
                for k in range(KT):
                    for t in range(ST):
                        last = transpose(ps_aux[:, k, t * P:(t + 1) * P], src[:, t, k * P:(k + 1) * P])
                last.then_inc(done, 1)

            def three(dst, w_hi, w_lo, a_hi, a_lo, start, stop, **kw):
                nc.tensor.matmul(dst, w_hi, a_hi, start=start, stop=False, **kw)
                nc.tensor.matmul(dst, w_hi, a_lo, start=False, stop=False, **kw)
                return nc.tensor.matmul(dst, w_lo, a_hi, start=False, stop=stop, **kw)

            def rows_product(dst, t, a_hi, a_lo, w_hi, w_lo, first, final):
                return three(dst[:, t, :], a_hi, a_lo, w_hi, w_lo, start=first and t % 2 == 0, stop=final,
                             skip_group_check=True)

            def up(i, s):
                k = step(i, s)
                w_hi, w_lo, a_hi, a_lo = (wup_hi, wup_lo, x1T_hi, x1T_lo) if s < PAIRS else (fup_hi, fup_lo, yT_hi, yT_lo)
                if s == 0:
                    pe.wait_ge(x1T_hid, i + 1)
                    pe.wait_ge(x1T_lod, i + 1)
                    if isinstance(i, int) and i == 0:
                        pe.wait_ge(prep_hi, 5)
                        pe.wait_ge(prep_lo, 5)
                if s == 1 and isinstance(i, int) and i == 0:
                    pe.wait_ge(prep_hi, 6)
                    pe.wait_ge(prep_lo, 6)
                if s == PAIRS:
                    pe.wait_ge(yT_hid, i)
                    pe.wait_ge(yT_lod, i)
                    if isinstance(i, int) and i == 1:
                        pe.wait_ge(flo_done, 1)
                if not isinstance(k, int) or k >= 2:
                    pe.wait_ge(act_done, k - 1)
                for h in range(2):
                    m = 2 * (s % PAIRS) + h
                    for c in range(KT):
                        last = three(ps_hid[:, s % 2, h, :], w_hi[:, c, m * P:(m + 1) * P],
                                     w_lo[:, c, m * P:(m + 1) * P], a_hi[:, c, :], a_lo[:, c, :],
                                     start=(c == 0), stop=(c == KT - 1))
                last.then_inc(up_done, 1)

            def down(i, s):
                k = step(i, s)
                w_hi, w_lo = (wdown_hi, wdown_lo) if s < PAIRS else (fdown_hi, fdown_lo)
                first, final = s % PAIRS == 0, s % PAIRS == PAIRS - 1
                if isinstance(i, int) and i == 0 and s == 0:
                    pe.wait_ge(fup_bias_made, 1)
                    pe.wait_ge(prep_hi, 6)
                    pe.wait_ge(prep_lo, 6)
                if s == 0 and (not isinstance(i, int) or i >= 2):
                    pe.wait_ge(z_done, i - 1)
                if s == PAIRS:
                    if isinstance(i, int) and i == G:
                        pe.wait_ge(z_done, i - 1)
                    else:
                        pe.wait_ge(x2_done, i + 1)
                    if isinstance(i, int) and i == 1:
                        pe.wait_ge(flo_done, 2)
                pe.wait_ge(act_done, k + 1)
                pe.wait_ge(lo_done, k + 1)
                very_last = isinstance(i, int) and i == G and final
                for bank in ((0, 1), (2, 3)) if very_last else (range(ST),):
                    for h in range(2):
                        m = 2 * (s % PAIRS) + h
                        for t in bank:
                            tile = slice(t * P, (t + 1) * P)
                            last = rows_product(ps_acc, t, hid_hi[:, s % 2, h, tile], hid_lo[:, s % 2, h, tile],
                                                w_hi[:, m, :], w_lo[:, m, :], first and h == 0, final and h == 1)
                    if very_last:
                        last.then_inc(last_bank, 1)
                if not very_last:
                    last.then_inc(down_done, 1)

            def iteration(i, par, on):
                n = i + 1
                first = isinstance(i, int) and i == -1

                second = isinstance(i, int) and i == 0

                def turn_x2n():
                    pe.wait_ge(x2n_done, n + 1)
                    pe.wait_ge(gated, n + 1)
                    turn_rows(x2n, x1T_ps)

                def turns(place):
                    if place == on.turn_y and on.ffn:
                        pe.wait_ge(yn_done, i)
                        turn_rows(yn, yT_ps)
                    if place == on.turn and on.front:
                        if on.ffn:
                            pe.wait_ge(yT_hid, i)
                            pe.wait_ge(yT_lod, i)
                        if isinstance(i, int) and i == 0:
                            pe.wait_ge(x1T_hid, 1)
                            pe.wait_ge(x1T_lod, 1)
                        pe.wait_ge(xn_done, n + 1)
                        turn_rows(xn, xT_ps)
                        if first:
                            turn_rest_rows()
                            couple_output()
                            turn_up_weights(0)
                    if place == on.beta and on.front:
                        pe.wait_ge(xT_hid, n + 1)
                        pe.wait_ge(xT_lod, n + 1)
                        for c in range(KT):
                            last = three(ps_aux[:, 0, :], win_hi[:, c, :], win_lo[:, c, :],
                                         xT_hi[:, c, :], xT_lo[:, c, :], start=(c == 0), stop=(c == KT - 1))
                        last.then_inc(beta_ps, 1)
                        if first:
                            spread_gate_bias()

                for s in range(SLOTS):
                    turns(s - 0.5)
                    if s in on.slots():
                        up(i, s)
                    turns(s)
                    if s == on.gate and on.front:
                        pe.wait_ge(rot_done, n + 1)
                        for c in range(KT):
                            for t in range(ST):
                                tile = slice(t * P, (t + 1) * P)
                                last = rows_product(aux_rows, t, xT_hi[:, c, tile], xT_lo[:, c, tile],
                                                    wgate_hi[:, c, :], wgate_lo[:, c, :], c == 0, c == KT - 1)
                        last.then_inc(gate_ps, 1)
                    if s == on.out and on.front:
                        pe.wait_ge(gate_pre, n + 1)
                        pe.wait_ge(turned_hid, n + 1)
                        pe.wait_ge(turned_lod, n + 1)
                        for t in range(ST):
                            tile = slice(t * P, (t + 1) * P)
                            last = rows_product(aux_rows, t, turned_hi[:, tile], turned_lo[:, tile],
                                                wout_hi[:, :], wout_lo[:, :], True, True)
                        last.then_inc(out_ps, 1)
                        if first:
                            turn_up_weights(1)
                            turn_down_weights(0)
                            ffn_bias()
                            turn_down_weights(1)
                    if s == on.turn2 and on.front and not second:
                        turn_x2n()
                    if s == 0 and on.final:
                        down(i - 1, SLOTS - 1)
                    elif s > 0 and s - 1 in on.slots():
                        down(i, s - 1)
                    if s == on.turn2 and second:
                        turn_x2n()

            run(pe, iteration)

        @block.scalar
        def _(act):
            def scaled(dst, src, scale=1.0, bias=0.0):
                return nc.scalar.activation(dst, src, ACT.Identity, scale=scale, bias=bias)

            def staged(b):
                return ps_hid[:, b, :, :].rearrange("p a n -> p (a n)")

            act.dma_start(raw_in, in_proj_w).then_inc(small_in, 16)
            act.dma_start(raw_gate, gate_w.rearrange("(e p) d -> p e d", p=P)).then_inc(small_in, 16)
            act.dma_start(raw_out, out_proj_w.rearrange("(e p) k -> p e k", p=P)).then_inc(small_in, 16)
            for part in range(2):
                act.dma_start(coup_raw[part * K:(part + 1) * K, :],
                              coupling.rearrange("h j k -> (h j) k")).then_inc(small_in, 16)
            act.wait_ge(const_made, 11)
            nc.scalar.activation(tiny[:, 7:8], eps_tile[:, 0:1], ACT.Silu).then_inc(z_scaled, 1)

            def small_weights():
                act.wait_ge(cols_done, 1)
                act.wait_ge(prep_T, 1)
                for k in range(KT):
                    scaled(win_hi[:, k, :], staged(0)[:, k * P:(k + 1) * P], col("n1_g", k))
                    last = scaled(wgate_hi[:, k, :], staged(0)[:, GT + k * D:GT + (k + 1) * D], col("n1_g", k))
                last.then_inc(prep_hi, 1)
                nc.scalar.activation(tiny[:, 5:6], col("log_decay"), ACT.Tanh, scale=0.5).then_inc(decay_tanh, 1)
                act.wait_ge(prep_T, 2)
                scaled(outT, staged(1)[:, 0:D], 0.5).then_inc(outT_done, 1)

            def gate_fans():
                act.wait_ge(gate_col_made, 1)
                for e in range(KT):
                    last = scaled(gate_fan[:, e, :], ident[:], 0.0, gate_col[:, e:e + 1])
                last.then_inc(fan_done, 1)

            def decay_row():
                act.wait_ge(decay_made, 1)
                scaled(decay[:], decay[:], 1.0, tiny[:, 6:7]).then_inc(decay_along, 1)

            def tables():
                act.wait_ge(tables_arg, 1)
                nc.scalar.activation(sin_t[:, 0:TAB], tab[2], ACT.Sin, scale=tiny[:, 4:5]).then_inc(tables_sin, 1)
                act.wait_ge(tables_arg, 2)
                nc.scalar.activation(cos_t[:, 0:TAB], tab[0], ACT.Sin, scale=TURN).then_inc(tables_sin, 1)

            def out_weights():
                act.wait_ge(prep_T, 3)
                scaled(wout_hi[:, :], staged(1)[:, GT:GT + D]).then_inc(prep_hi, 1)

            def up_weights(k):
                act.wait_ge(cols_done, 2)
                act.wait_ge(prep_T, 4 + k)
                scaled(wup_hi[:, k, :], staged(k), col("n2_g", k)).then_inc(prep_hi, 1)

            def down_weights(half):
                act.wait_ge(prep_T, 6 + half)
                scaled(wdown_hi[:, half * MT // 2:(half + 1) * MT // 2, :].rearrange("p c d -> p (c d)"),
                       staged(half)).then_inc(prep_hi, 1)

            def centre(w, loaded):
                act.wait_ge(loaded, 16)
                scaled(w, w.bitcast(I32), 1.0, zero_point[:, :]).then_inc(centred, 1)

            def ffn_up_weights():
                act.wait_ge(deq_done, 1)
                for k in range(KT):
                    last = scaled(fup_hi[:, k, :], ffn_up[:, k * M:(k + 1) * M], col("gamma", k))
                last.then_inc(fhi_done, 1)

            def ffn_down_weights():
                act.wait_ge(deq_done, 2)
                scaled(fdown_hi[:, :, :].rearrange("p c d -> p (c d)"), ffn_down, 0.5).then_inc(fhi_done, 1)

            def norm_rows(dst, src, st, done):
                for t in range(ST):
                    last = scaled(dst[:, t, :], src[:, t, :], st.r[:, t:t + 1], st.shift[:, t:t + 1])
                last.then_inc(done, 1)

            def high(dst, done):
                scaled(dst[:, :, :].rearrange("p a n -> p (a n)"),
                       ps_aux[:, :, :].rearrange("p a n -> p (a n)")).then_inc(done, 1)

            def activate(i, s):
                k = step(i, s)
                bias = up_bias if s < PAIRS else fup_bias
                act.wait_ge(up_done, k + 1)
                if not isinstance(k, int) or k >= 1:
                    act.wait_ge(lo_done, k)
                if not isinstance(k, int) or k >= 2:
                    act.wait_ge(down_done, k - 1)
                for h in range(2):
                    m = 2 * (s % PAIRS) + h
                    nc.scalar.activation(hid[:, h, :], ps_hid[:, s % 2, h, :], ACT.Silu, bias=bias[:, m:m + 1])
                    last = nc.scalar.activation(hid_hi[:, s % 2, h, :], ps_hid[:, s % 2, h, :], ACT.Silu,
                                                bias=bias[:, m:m + 1])
                last.then_inc(act_done, 1)

            def iteration(i, par, on):
                n = i + 1
                first = isinstance(i, int) and i == -1
                second = isinstance(i, int) and i == 0
                third = isinstance(i, int) and i == 1
                last_mlp = isinstance(i, int) and i == G - 1
                last_one = isinstance(i, int) and i == G + 1

                def norm_x():
                    act.wait_ge(st_x.done, n + 1)
                    if not isinstance(n, int) or n >= 1:
                        act.wait_ge(x1_done, n)
                    norm_rows(xn, x_in[:, 1 - par, :, :], st_x, xn_done)

                def turns(place):
                    if place == on.turn_y and on.ffn:
                        act.wait_ge(yT_ps, i)
                        high(yT_hi, yT_hid)
                        if third:
                            norm_x()
                    if place == on.turn and on.front:
                        act.wait_ge(xT_ps, n + 1)
                        high(xT_hi, xT_hid)
                        if first:
                            out_weights()
                            up_weights(0)
                            decay_row()
                            tables()
                            gate_fans()
                            centre(ffn_up[:, :], q1_in)

                def norm_y(m, p):
                    act.wait_ge(st_y.done, m + 1)
                    if not isinstance(m, int) or m >= 1:
                        act.wait_ge(zb_done, m)
                    norm_rows(yn, y[p], st_y, yn_done)

                for s in range(SLOTS):
                    turns(s - 0.5)
                    if s == 0 and second:
                        act.wait_ge(up_bias_made, 1)
                    if s == on.turn2 and on.front:
                        act.wait_ge(x1T_ps, n + 1)
                        high(x1T_hi, x1T_hid)
                        if first:
                            down_weights(1)
                    if s == PAIRS and isinstance(i, int) and i == 1:
                        act.wait_ge(fup_bias_made, 1)
                    if s in on.slots():
                        activate(i, s)
                    if s == 0:
                        turns(s)
                    if s == 0 and on.front and not second and not third:
                        norm_x()
                        if first:
                            small_weights()
                    if s > 0:
                        turns(s)
                    if s == 1 and third:
                        norm_y(0, 0)
                    if s == on.close and last_one:
                        for t in range(ST):
                            act.wait_ge(last_sum, t + 1)
                            scaled(zb[:, t, :], zb[:, t, :], 1.0, st_z.neg[:, t:t + 1]).then_inc(out_done, 1)
                    elif s == on.close and on.final:
                        act.wait_ge(z_shift, i - 1)
                        for t in range(ST):
                            last = scaled(zb[:, t, :], zb[:, t, :], st_z.r[:, t:t + 1], st_z.neg[:, t:t + 1])
                        last.then_inc(z_scaled, 1)
                    if s == on.gate and on.front:
                        act.wait_ge(back_done, n + 1)
                        scaled(turned_hi[:, :], rot[:, 0, :]).then_inc(turned_hid, 1)
                        act.wait_ge(gate_pre, n + 1)
                        nc.scalar.activation(gate[:, :, :], gate[:, :, :], ACT.Tanh, scale=0.5).then_inc(gate_done, 1)
                        if first:
                            up_weights(1)
                            down_weights(0)
                            centre(ffn_down, q2_in)
                            ffn_up_weights()
                    if s == on.norm and on.front:
                        act.wait_ge(st_1.done, n + 1)
                        norm_rows(x2n, x1, st_1, x2n_done)
                        if first:
                            act.wait_ge(st_x.done, 2)
                            norm_rows(xn, x_in[:, 1, :, :], st_x, xn_done)
                        if second:
                            ffn_down_weights()
                    if s == (6 if last_mlp else 7) and on.mlp and not second:
                        norm_y(i, par)

            run(act, iteration)

        @block.vector
        def _(dve):
            made = [0]

            def link(ins):
                made[0] += 1
                ins.then_inc(dve_setup, 1)
                dve.wait_ge(dve_setup, made[0])

            def staged(b):
                return ps_hid[:, b, :, :].rearrange("p a n -> p (a n)")

            def stats(st, src, n):
                if not isinstance(n, int) or n >= 1:
                    dve.wait_ge(st.done, n + st.ahead)
                for t in range(ST):
                    last = nc.vector.bn_stats(st.raw[:, t, :], src[:, t, :])
                last.then_inc(st.bn, 1)
                aggregate(st, n)

            def aggregate(st, n):
                dve.wait_ge(dve_setup, 1)
                dve.wait_ge(st.bn, n + 1)
                for t in range(ST):
                    last = nc.vector.bn_aggr(st.mv[:, t, :], st.raw[:, t, :])
                last.then_inc(st.agg, 1)

            link(nc.vector.memset(decay[:], 0.0))
            dve.wait_ge(x_loaded, 16)
            stats(st_x, x_in[:, 0, :, :], 0)
            dve.wait_ge(cols_ps, 1)
            nc.vector.tensor_copy(vec_cols[:, 0:NEARLY], ps_acc[:, 0, 0:NEARLY]).then_inc(cols_done, 1)
            dve.wait_ge(cols_done, 1)
            turns, whole, coarse, fine = (tiny[:, k:k + 1] for k in range(4))
            link(nc.vector.tensor_scalar(turns, col("frequency"), INV_TWO_PI, None, ALU.mult))
            link(nc.vector.tensor_scalar(whole, turns, ROUND_TO_INT, -ROUND_TO_INT, ALU.add, ALU.add))
            link(nc.vector.tensor_tensor(turns, turns, whole, ALU.subtract))
            link(nc.vector.tensor_scalar(coarse, turns, ROUND_TO_13_BITS, -ROUND_TO_13_BITS, ALU.add, ALU.add))
            link(nc.vector.tensor_tensor(fine, turns, coarse, ALU.subtract))

            def dot(k, src, vec):
                link(nc.vector.tensor_tensor_reduce(out=junk, in0=src, in1=vec, scale=1.0, scalar=0.0,
                                                    op0=ALU.mult, op1=ALU.add, accum_out=dots[:, k:k + 1]))

            def low(dst, src, scale, hi, done=None):
                last = nc.vector.scalar_tensor_tensor(out=dst, in0=src, scalar=scale, in1=hi.bitcast(F32),
                                                      op0=ALU.mult, op1=ALU.subtract)
                if done:
                    last.then_inc(done, 1)

            dve.wait_ge(small_in, 16 * 5)
            dve.wait_ge(bc_in, 16)
            dot(0, raw_in, n1_b_bc)
            dve.wait_ge(const_made, 11)
            pos = cos_t[:, 0:TAB]
            link(nc.vector.tensor_scalar(tab[0], pos, coarse, None, ALU.mult))
            link(nc.vector.tensor_scalar(tab[1], tab[0], ROUND_TO_INT, -ROUND_TO_INT, ALU.add, ALU.add))
            link(nc.vector.tensor_tensor(tab[0], tab[0], tab[1], ALU.subtract))
            dve.wait_ge(prep_hi, 1)
            for k in range(KT):
                low(win_lo[:, k, :], staged(0)[:, k * P:(k + 1) * P], col("n1_g", k), win_hi[:, k, :])
                low(wgate_lo[:, k, :], staged(0)[:, GT + k * D:GT + (k + 1) * D], col("n1_g", k),
                    wgate_hi[:, k, :], prep_lo if k == KT - 1 else None)
            def small_sums():
                for e in range(KT):
                    dot(1 + e, raw_gate[:, e, :], n1_b_bc)
                a = cols["gate_b"][0]
                nc.vector.tensor_tensor(gate_col[:], dots[:, 1:1 + KT], vec_cols[:, a:a + KT],
                                        ALU.add).then_inc(gate_col_made, 1)

            def gate_bias_rows():
                dve.wait_ge(gate_bias_ps, 1)
                nc.vector.tensor_copy(gate_bias[:], ps_acc[:, 1, 0:D]).then_inc(gate_bias_made, 1)
                dve.wait_ge(gate_bias_made, 1)

            def rest_columns():
                dve.wait_ge(cols_ps, 2)
                nc.vector.tensor_copy(vec_cols[:, NEARLY:NROW], ps_acc[:, 2, 0:NREST]).then_inc(cols_done, 1)
                dve.wait_ge(cols_done, 2)

            def tables():
                link(nc.vector.scalar_tensor_tensor(out=tab[0], in0=pos, scalar=fine, in1=tab[0],
                                                    op0=ALU.mult, op1=ALU.add))
                link(nc.vector.tensor_scalar(tab[1], tab[0], ROUND_TO_INT, -ROUND_TO_INT, ALU.add, ALU.add))
                nc.vector.tensor_tensor(tab[2], tab[0], tab[1], ALU.subtract).then_inc(tables_arg, 1)
                dve.wait_ge(tables_arg, 1)
                link(nc.vector.tensor_scalar(tab[0], tab[0], 0.25, None, ALU.add))
                link(nc.vector.tensor_scalar(tab[1], tab[0], ROUND_TO_INT, -ROUND_TO_INT, ALU.add, ALU.add))
                nc.vector.tensor_tensor(tab[0], tab[0], tab[1], ALU.subtract).then_inc(tables_arg, 1)

            def decay_value():
                dve.wait_ge(decay_tanh, 1)
                nc.vector.tensor_scalar(tiny[:, 6:7], tiny[:, 5:6], 0.5, 0.5, ALU.mult, ALU.add).then_inc(decay_made, 1)

            def out_weights():
                dve.wait_ge(prep_hi, 2)
                low(wout_lo[:, :], staged(1)[:, GT:GT + D], 1.0, wout_hi[:, :], prep_lo)

            def up_weights(k):
                dve.wait_ge(prep_hi, 3 + k)
                low(wup_lo[:, k, :], staged(k), col("n2_g", k), wup_hi[:, k, :], prep_lo)

            def up_biases():
                dve.wait_ge(w1_in, 32)
                dve.wait_ge(rest_bc_in, 16 * 3)
                for m in range(MT):
                    dot(1 + KT + m, w1_rows(m), n2_b_bc)
                a = cols["b1"][0]
                nc.vector.tensor_tensor(up_bias[:], dots[:, 1 + KT:], vec_cols[:, a:a + MT],
                                        ALU.add).then_inc(up_bias_made, 1)

            def down_weights(half):
                dve.wait_ge(prep_hi, 5 + half)
                part = slice(half * MT // 2, (half + 1) * MT // 2)
                low(wdown_lo[:, part, :].rearrange("p c d -> p (c d)"), staged(half), 1.0,
                    wdown_hi[:, part, :].rearrange("p c d -> p (c d)"), prep_lo)

            def save_starts():
                dve.wait_ge(tables_sin, 2)
                nc.vector.tensor_copy(starts[:, 0, :], cos_t[:, GT:TAB])
                nc.vector.tensor_copy(starts[:, 1, :], sin_t[:, GT:TAB]).then_inc(starts_done, 1)

            def later_table(q):
                if q == 1:
                    dve.wait_ge(starts_done, 1)
                c0, s0 = cos_t[:, 0:GT], sin_t[:, 0:GT]
                part = slice(q * GT, (q + 1) * GT)
                c, s_ = starts[:, 0, q:q + 1], starts[:, 1, q:q + 1]
                nc.vector.tensor_scalar(rot[:, 0, :], s0, s_, None, ALU.mult)
                link(nc.vector.tensor_scalar(rot[:, 1, :], c0, s_, None, ALU.mult))
                nc.vector.scalar_tensor_tensor(out=cos_t[:, part], in0=c0, scalar=c, in1=rot[:, 0, :],
                                               op0=ALU.mult, op1=ALU.subtract)
                link(nc.vector.scalar_tensor_tensor(out=sin_t[:, part], in0=s0, scalar=c, in1=rot[:, 1, :],
                                                    op0=ALU.mult, op1=ALU.add))

            def ffn_up_weights():
                dve.wait_ge(fhi_done, 1)
                for k in range(KT):
                    low(fup_lo[:, k, :], ffn_up[:, k * M:(k + 1) * M], col("gamma", k), fup_hi[:, k, :],
                        flo_done if k == KT - 1 else None)

            def ffn_up_bias():
                dve.wait_ge(fbias_ps, 1)
                b = cols["fb1"][0]
                nc.vector.tensor_tensor(fup_bias[:], ps_acc[:, 0, 0:MT], vec_cols[:, b:b + MT],
                                        ALU.add).then_inc(fup_bias_made, 1)

            def ffn_down_weights():
                dve.wait_ge(fhi_done, 2)
                low(fdown_lo[:, :, :].rearrange("p c d -> p (c d)"), ffn_down, 0.5,
                    fdown_hi[:, :, :].rearrange("p c d -> p (c d)"), flo_done)

            def wide(buf):
                return buf.rearrange("p a n -> p (a n)")

            def low_of_aux(dst, hi, done):
                nc.vector.tensor_tensor(wide(dst[:, :, :]), wide(ps_aux[:, :, :]),
                                        wide(hi[:, :, :]).bitcast(F32), ALU.subtract).then_inc(done, 1)

            def low_of_hidden(i, s):
                k = step(i, s)
                dve.wait_ge(act_done, k + 1)
                if not isinstance(k, int) or k >= 2:
                    dve.wait_ge(down_done, k - 1)
                nc.vector.tensor_tensor(wide(hid_lo[:, s % 2, :, :]), wide(hid),
                                        wide(hid_hi[:, s % 2, :, :]).bitcast(F32),
                                        ALU.subtract).then_inc(lo_done, 1)

            def iteration(i, par, on):
                n = i + 1
                first = isinstance(i, int) and i == -1
                second = isinstance(i, int) and i == 0
                third = isinstance(i, int) and i == 1
                last_mlp = isinstance(i, int) and i == G - 1

                def recur():
                    if isinstance(n, int):
                        table = slice(n % GB * GT, (n % GB + 1) * GT)
                        place = slice(n % GB, n % GB + 1)
                    else:
                        table = bass.ts(n % GB, GT)
                        place = bass.ts(n % GB, 1)
                    halves = ((slice(0, K), slice(K, K2)), (slice(K, K2), slice(0, K)))
                    dve.wait_ge(beta_ps, n + 1)
                    nc.vector.scalar_tensor_tensor(out=rot[:, 0, :], in0=ps_aux[:, 0, :], scalar=beta_bias,
                                                   in1=cos_t[:, table], op0=ALU.add, op1=ALU.mult)
                    for to, of in halves:
                        last = nc.vector.scalar_tensor_tensor(
                            out=rot[to, 1, :], in0=ps_aux[of, 0, :], scalar=beta_bias[of, :],
                            in1=sin_t[of, table], op0=ALU.add, op1=ALU.mult)
                    last.then_inc(rot_done, 1)
                    if second:
                        low_of_hidden(0, 0)
                    dve.wait_ge(rot_done, n + 1)
                    nc.vector.tensor_tensor(rot[:, 0, :], rot[:, 0, :], rot[:, 1, :],
                                            ALU.add).then_inc(turned_in, 1)
                    if isinstance(n, int) and n == 0:
                        start = 0.0
                    else:
                        nc.vector.tensor_tensor(carry[:], scanned[:, GT - 1:GT], carry_mask[:, place],
                                                ALU.mult).then_inc(carry_done, 1)
                        dve.wait_ge(carry_done, n)
                        start = carry[:]
                    dve.wait_ge(turned_in, n + 1)
                    nc.vector.tensor_tensor_scan(scanned[:], decay[:], rot[:, 0, :], start, ALU.mult,
                                                 ALU.add).then_inc(scan_done, 1)
                    dve.wait_ge(scan_done, n + 1)
                    nc.vector.tensor_tensor(rot[:, 0, :], scanned[:], cos_t[:, table], ALU.mult)
                    for to, of in halves:
                        last = nc.vector.tensor_tensor(rot[to, 1, :], scanned[of, :], sin_t[of, table], ALU.mult)
                    last.then_inc(back_parts, 1)
                    dve.wait_ge(back_parts, n + 1)
                    nc.vector.tensor_tensor(rot[:, 0, :], rot[:, 0, :], rot[:, 1, :],
                                            ALU.subtract).then_inc(back_done, 1)

                def low_of_x1T():
                    dve.wait_ge(x1T_hid, n + 1)
                    low_of_aux(x1T_lo, x1T_hi, x1T_lod)

                def turns(place):
                    if place == on.turn_y and on.ffn:
                        dve.wait_ge(yT_hid, i)
                        low_of_aux(yT_lo, yT_hi, yT_lod)
                    if place == on.turn and on.front:
                        dve.wait_ge(xT_hid, n + 1)
                        low_of_aux(xT_lo, xT_hi, xT_lod)
                        if first:
                            rest_columns()
                            decay_value()
                            tables()
                            small_sums()
                            save_starts()
                            dve.wait_ge(decay_along, 1)
                    if place == on.beta and on.front:
                        recur()

                def add_y(m, p):
                    dve.wait_ge(st_2.done, m + 1)
                    if on.final:
                        dve.wait_ge(out_done, m - 1)
                    for t in range(ST):
                        last = nc.vector.scalar_tensor_tensor(
                            out=y[p][:, t, :], in0=x1b[:, t, :], scalar=st_2.r[:, t:t + 1],
                            in1=x_in[:, p, t, :], op0=ALU.mult, op1=ALU.add)
                    last.then_inc(y_done, 1)

                def stats_of_y(m, p):
                    dve.wait_ge(y_done, m + 1)
                    stats(st_y, y[p], m)

                def stats_of_next(m, p):
                    dve.wait_ge(x_loaded, 16 * (m + 3))
                    stats(st_x, x_in[:, p, :, :], m + 2)

                last_mlp = isinstance(i, int) and i == G - 1

                for s in range(SLOTS):
                    turns(s - 0.5)
                    if s == 0 and second:
                        later_table(1)
                    if s == 3 and third:
                        later_table(2)
                    if s == 0 and third:
                        add_y(0, 0)
                    if s == on.turn2 and on.front and not second:
                        low_of_x1T()
                    if s in on.slots() and not (second and s in (0, on.out)):
                        low_of_hidden(i, s)
                    if s == 0 and third:
                        stats_of_y(0, 0)
                    if s == 1 and third:
                        stats_of_next(0, 0)
                        ffn_down_weights()
                    if s == 0:
                        turns(s)
                    if s == 0 and on.final:
                        if isinstance(i, int) and i == G + 1:
                            dve.wait_ge(st_z.done, G - 1 + st_z.ahead)
                            for b in range(2):
                                rows = slice(2 * b, 2 * b + 2)
                                dve.wait_ge(last_bank, b + 1)
                                nc.vector.tensor_tensor(zb[:, rows, :], ps_acc[:, rows, :], zb[:, rows, :],
                                                        ALU.add).then_inc(z_done, 1)
                                dve.wait_ge(z_done, G + b)
                                for t in (2 * b, 2 * b + 1):
                                    last = nc.vector.bn_stats(st_z.raw[:, t, :], zb[:, t, :])
                            last.then_inc(st_z.bn, 1)
                            aggregate(st_z, i - 2)
                        else:
                            dve.wait_ge(down_done, step(i - 1, SLOTS - 1) + 1)
                            nc.vector.tensor_tensor(zb, ps_acc[:, :, :], zb, ALU.add).then_inc(z_done, 1)
                            dve.wait_ge(z_done, i - 1)
                            stats(st_z, zb, i - 2)
                        if isinstance(i, int) and i == G + 1:
                            dve.wait_ge(z_shift, G)
                            for t in range(ST):
                                nc.vector.scalar_tensor_tensor(
                                    out=zb[:, t, :], in0=zb[:, t, :], scalar=st_z.r[:, t:t + 1],
                                    in1=y[par][:, t, :], op0=ALU.mult, op1=ALU.add).then_inc(last_sum, 1)
                    if s > 0:
                        turns(s)
                    if s == on.gate and on.front:
                        if first:
                            out_weights()
                        dve.wait_ge(turned_hid, n + 1)
                        nc.vector.tensor_tensor(turned_lo[:, :], rot[:, 0, :], turned_hi[:, :].bitcast(F32),
                                                ALU.subtract).then_inc(turned_lod, 1)
                        dve.wait_ge(gate_ps, n + 1)
                        if first:
                            gate_bias_rows()
                        nc.vector.tensor_tensor(gate[:, :, :], aux_rows, over_rows(gate_bias[:]),
                                                ALU.add).then_inc(gate_pre, 1)
                        if first:
                            up_weights(0)
                    if s == on.out and on.front:
                        dve.wait_ge(gate_done, n + 1)
                        dve.wait_ge(out_ps, n + 1)
                        nc.vector.scalar_tensor_tensor(out=gate[:, :, :], in0=gate[:, :, :], scalar=1.0,
                                                       in1=aux_rows, op0=ALU.add, op1=ALU.mult).then_inc(gated, 1)
                    if s == 3 and second:
                        ffn_up_weights()
                    if s == 4 and on.mlp:
                        dve.wait_ge(down_done, step(i, PAIRS - 1) + 1)
                        dve.wait_ge(x1b_done, i + 1)
                        nc.vector.tensor_tensor(x1b, ps_acc[:, :, :], x1b, ALU.add).then_inc(x2_done, 1)
                    if s == (on.gate if on.mlp else PAIRS + 2) and on.ffn:
                        dve.wait_ge(st_y.ratiod, i)
                        if on.final:
                            dve.wait_ge(stored, 16 * (i - 1))
                        for t in range(ST):
                            last = nc.vector.scalar_tensor_tensor(
                                out=zb[:, t, :], in0=yn[:, t, :], scalar=st_y.ratio[:, t:t + 1],
                                in1=fc2_half[:], op0=ALU.mult, op1=ALU.add)
                        last.then_inc(zb_done, 1)
                    if s == on.turn2 and second:
                        low_of_x1T()
                    if s == on.out and on.front:
                        dve.wait_ge(st_x.ratiod, n + 1)
                        dve.wait_ge(gated, n + 1)
                        if on.mlp:
                            dve.wait_ge(x1b_done, n)
                            dve.wait_ge(x2n_done, n)
                        for t in range(ST):
                            last = nc.vector.scalar_tensor_tensor(
                                out=x1[:, t, :], in0=xn[:, t, :], scalar=st_x.ratio[:, t:t + 1],
                                in1=gate[:, t, :], op0=ALU.mult, op1=ALU.add)
                        last.then_inc(x1_done, 1)
                        dve.wait_ge(x1_done, n + 1)
                        if second:
                            low_of_hidden(i, s)
                        stats(st_1, x1, n)
                        if first:
                            up_weights(1)
                            dve.wait_ge(x_loaded, 16 * 2)
                            stats(st_x, x_in[:, 1, :, :], 1)
                            down_weights(0)
                    if s == (4 if last_mlp else 5) and on.mlp:
                        dve.wait_ge(x2_done, i + 1)
                        stats(st_2, x1b, i)
                        if second:
                            link(nc.vector.tensor_scalar(fc2_half[:], fc2_b_bc, 0.5, None, ALU.mult))
                    if s == (6 if third else 5) and on.mlp and not second:
                        add_y(i, par)
                    if s == (5 if last_mlp else 6) and on.mlp and not second:
                        stats_of_y(i, par)
                    if s == 7 and first:
                        down_weights(1)
                        up_biases()
                        ffn_up_bias()
                    if s == 7 and on.next_stat and not first and not second:
                        stats_of_next(i, par)
                    if s == 7 and third:
                        later_table(3)

            run(dve, iteration)


_INS = ["L0_attn_x", "L0_attn_in_proj_w", "L0_attn_log_decay", "L0_attn_frequency", "L0_attn_coupling",
        "L0_attn_out_proj_w", "L0_attn_gate_w", "L0_attn_gate_b", "L0_attn_n1_g", "L0_attn_n1_b",
        "L0_attn_n2_g", "L0_attn_n2_b", "L0_attn_mlp_w1", "L0_attn_mlp_b1", "L0_attn_mlp_w2", "L0_attn_mlp_b2",
        "L0_ffn_ln_gamma", "L0_ffn_ln_beta", "L0_ffn_fc1_q", "L0_ffn_fc1_scales", "L0_ffn_fc1_bias",
        "L0_ffn_fc2_q", "L0_ffn_fc2_scales", "L0_ffn_fc2_bias"]


def kernel(**inputs):
    import numpy as np
    import concourse.bacc as bacc
    from concourse.bass_utils import run_bass_kernel_spmd

    nc = bacc.Bacc("TRN2", target_bir_lowering=False, num_devices=1)
    arrays, args = {}, []
    for name in _INS:
        a = np.ascontiguousarray(inputs[name])
        arrays[f"in_{name}"] = a
        args.append(nc.dram_tensor(f"in_{name}", a.shape, mybir.dt.from_np(a.dtype), kind="ExternalInput").ap())
    shape = arrays["in_L0_attn_x"].shape
    out = nc.dram_tensor("out", shape, F32, kind="ExternalOutput").ap()
    build(nc, *args, out)
    r = run_bass_kernel_spmd(nc, [arrays], core_ids=[0])
    return r.results[0]["out"]
```
